# Optimizing a Trainium2 kernel written in Bass

```python
import numpy as np
import jax
import jax.numpy as jnp

def _softmax(x, axis=-1):
    return jax.nn.softmax(x, axis=axis)

def _gelu(x):
    return jax.nn.gelu(x, approximate=True)

def _silu(x):
    return jax.nn.silu(x)

def _sigmoid(x):
    return jax.nn.sigmoid(x)

def _layernorm(x, axis=-1, eps=1e-05):
    m = jnp.mean(x, axis=axis, keepdims=True)
    v = jnp.var(x, axis=axis, keepdims=True)
    return (x - m) / jnp.sqrt(v + eps)

def _scatter_add(tgt, idx, src, axis=0):
    return tgt.at[idx].add(src)

def _segment_sum(src, seg, n):
    return jax.ops.segment_sum(src, seg, n)
kernel_name = 'mk_hybrid_d1_jaxref_r4_5aaeb0'

def setup_inputs(seed: int=0):
    np.random.seed(seed)
    _w = jnp.asarray

    def _L0_attn_a_setup():
        import math
        import jax, jax.numpy as jnp
        import numpy as np
        N_HEADS = 16
        D_EMBED = 256
        key = jax.random.key(seed)
        ks = jax.random.split(key, 5)
        b, l, d = (2, 512, D_EMBED)
        return {'x': jax.random.normal(ks[0], (b, l, d), dtype=jnp.float32), 'w_in': jax.random.normal(ks[1], (3 * d, d), dtype=jnp.float32) * 0.02, 'b_in': jax.random.normal(ks[2], (3 * d,), dtype=jnp.float32) * 0.02, 'w_out': jax.random.normal(ks[3], (d, d), dtype=jnp.float32) * 0.02, 'b_out': jax.random.normal(ks[4], (d,), dtype=jnp.float32) * 0.02}
    _L0_attn_a_in = _L0_attn_a_setup()

    def _L0_attn_b_setup():
        import jax, jax.numpy as jnp
        import numpy as np
        B, T, D, H = (4, 256, 256, 16)
        key = jax.random.key(seed)
        ks = jax.random.split(key, 7)
        x = jax.random.normal(ks[0], (B, T, D), dtype=jnp.float32)
        scale = 0.02
        Wq = jax.random.normal(ks[1], (D, D), dtype=jnp.float32) * scale
        Wk = jax.random.normal(ks[2], (D, D), dtype=jnp.float32) * scale
        Wv = jax.random.normal(ks[3], (D, D), dtype=jnp.float32) * scale
        bq = jax.random.normal(ks[4], (D,), dtype=jnp.float32) * scale
        bk = jax.random.normal(ks[5], (D,), dtype=jnp.float32) * scale
        bv = jax.random.normal(ks[6], (D,), dtype=jnp.float32) * scale
        temperature = jnp.ones((H, 1, 1), dtype=jnp.float32)
        return {'x': x, 'Wq': Wq, 'bq': bq, 'Wk': Wk, 'bk': bk, 'Wv': Wv, 'bv': bv, 'temperature': temperature}
    _L0_attn_b_in = _L0_attn_b_setup()

    def _L0_ffn_setup():
        import jax, jax.numpy as jnp
        import numpy as np
        import math
        BETA = 0.9
        THRESHOLD = 1.0
        NUM_STEPS = 5
        ALPHA = 2.0

        @jax.custom_vjp
        def spike_fn(u):
            return (u > 0).astype(u.dtype)

        def _spike_fwd(u):
            return (spike_fn(u), u)

        def _spike_bwd(u, g):
            s = jnp.pi / 2.0 * ALPHA * u
            return (g * (ALPHA / 2.0) / (1.0 + s * s),)
        spike_fn.defvjp(_spike_fwd, _spike_bwd)
        key = jax.random.key(seed)
        k1, k2, k3 = jax.random.split(key, 3)
        n_embd = 256
        x = jax.random.normal(k1, (4, 512, n_embd), dtype=jnp.float32)
        W_fc = jax.random.normal(k2, (4 * n_embd, n_embd), dtype=jnp.float32) / math.sqrt(n_embd)
        W_proj = jax.random.normal(k3, (n_embd, 4 * n_embd), dtype=jnp.float32) / math.sqrt(4 * n_embd)
        return {'x': x, 'W_fc': W_fc, 'W_proj': W_proj}
    _L0_ffn_in = _L0_ffn_setup()
    _d = {'L0_attn_a_x': _L0_attn_a_in['x'], 'L0_attn_a_w_in': _L0_attn_a_in['w_in'], 'L0_attn_a_b_in': _L0_attn_a_in['b_in'], 'L0_attn_a_w_out': _L0_attn_a_in['w_out'], 'L0_attn_a_b_out': _L0_attn_a_in['b_out'], 'L0_attn_b_Wq': _L0_attn_b_in['Wq'], 'L0_attn_b_bq': _L0_attn_b_in['bq'], 'L0_attn_b_Wk': _L0_attn_b_in['Wk'], 'L0_attn_b_bk': _L0_attn_b_in['bk'], 'L0_attn_b_Wv': _L0_attn_b_in['Wv'], 'L0_attn_b_bv': _L0_attn_b_in['bv'], 'L0_attn_b_temperature': _L0_attn_b_in['temperature'], 'L0_ffn_W_fc': _L0_ffn_in['W_fc'], 'L0_ffn_W_proj': _L0_ffn_in['W_proj']}
    _x0 = _d['L0_attn_a_x']
    _d['L0_attn_a_x'] = jax.random.normal(jax.random.fold_in(jax.random.key(seed), 1), (2, 2048, 256), dtype=_x0.dtype)
    del _x0
    return _d

def reference(L0_attn_a_x, L0_attn_a_w_in, L0_attn_a_b_in, L0_attn_a_w_out, L0_attn_a_b_out, L0_attn_b_Wq, L0_attn_b_bq, L0_attn_b_Wk, L0_attn_b_bk, L0_attn_b_Wv, L0_attn_b_bv, L0_attn_b_temperature, L0_ffn_W_fc, L0_ffn_W_proj):

    def _L0_attn_a_ref(x, w_in, b_in, w_out, b_out):
        import math
        import jax, jax.numpy as jnp
        import numpy as np
        N_HEADS = 16
        D_EMBED = 256
        b, l, d = x.shape
        h = N_HEADS
        scale = 1.0 / math.sqrt(d // h)
        x_proj = (x @ w_in.T + b_in).reshape(b, l, h, -1)
        q, k, v = jnp.split(x_proj, 3, axis=-1)
        att = jnp.einsum('blhd,bmhd->blmh', q, k) * scale
        att = jax.nn.softmax(att, axis=2)
        opt = jnp.einsum('blmh,blhd->blhd', att, v).reshape(b, l, d)
        return opt @ w_out.T + b_out

    def _L0_attn_b_ref(x, Wq, bq, Wk, bk, Wv, bv, temperature):
        import jax, jax.numpy as jnp
        import numpy as np
        B, T, D, H = (4, 256, 256, 16)
        b, t, d = x.shape
        h = temperature.shape[0]
        dh = d // h
        q = (x @ Wq + bq).reshape(b, h, dh, t)
        k = (x @ Wk + bk).reshape(b, h, dh, t)
        v = (x @ Wv + bv).reshape(b, h, dh, t)
        attn = jnp.einsum('bhdt,bhds->bhts', k, v) * temperature
        attn = jax.nn.softmax(attn, axis=-1)
        out = jnp.einsum('bhdt,bhts->bhds', q, attn)
        return out.reshape(b, t, d)

    def _L0_ffn_ref(x, W_fc, W_proj):
        import jax, jax.numpy as jnp
        import numpy as np
        import math
        BETA = 0.9
        THRESHOLD = 1.0
        NUM_STEPS = 5
        ALPHA = 2.0

        @jax.custom_vjp
        def spike_fn(u):
            return (u > 0).astype(u.dtype)

        def _spike_fwd(u):
            return (spike_fn(u), u)

        def _spike_bwd(u, g):
            s = jnp.pi / 2.0 * ALPHA * u
            return (g * (ALPHA / 2.0) / (1.0 + s * s),)
        spike_fn.defvjp(_spike_fwd, _spike_bwd)
        h = jnp.square(jax.nn.relu(jnp.einsum('bsd,fd->bsf', x, W_fc)))
        y = jnp.einsum('bsf,df->bsd', h, W_proj)

        def step(mem, _):
            reset = jax.lax.stop_gradient(spike_fn(mem - THRESHOLD))
            mem_new = BETA * mem + y - reset * THRESHOLD
            spk = spike_fn(mem_new - THRESHOLD)
            return (mem_new, spk)
        mem0 = jnp.zeros_like(y)
        _, spks = jax.lax.scan(step, mem0, None, length=NUM_STEPS)
        return jnp.sum(spks, axis=0) / NUM_STEPS
    x = L0_attn_a_x
    x = x + _L0_attn_a_ref(_layernorm(x, axis=-1), L0_attn_a_w_in, L0_attn_a_b_in, L0_attn_a_w_out, L0_attn_a_b_out)
    x = x + _L0_ffn_ref(_layernorm(x, axis=-1), L0_ffn_W_fc, L0_ffn_W_proj)
    x = x + _L0_attn_b_ref(_layernorm(x, axis=-1), L0_attn_b_Wq, L0_attn_b_bq, L0_attn_b_Wk, L0_attn_b_bk, L0_attn_b_Wv, L0_attn_b_bv, L0_attn_b_temperature)
    x = x + _L0_ffn_ref(_layernorm(x, axis=-1), L0_ffn_W_fc, L0_ffn_W_proj)
    return x

_drawn_inputs = setup_inputs


def setup_inputs(seed=0):
    import zlib

    import numpy as np

    out = dict(_drawn_inputs(seed))
    spreads = {'L0_attn_b_temperature': (1.0, 0.6)}
    factors = {'L0_attn_a_b_in': 2.733,
     'L0_attn_b_Wq': 6.033,
     'L0_attn_b_bq': 8.0,
     'L0_attn_b_Wk': 7.523,
     'L0_attn_b_bk': 8.0,
     'L0_attn_b_Wv': 7.615,
     'L0_attn_b_bv': 8.0}
    for name, (base, spread) in spreads.items():
        noise = np.random.default_rng([zlib.crc32(name.encode()), seed]).standard_normal(out[name].shape)
        drawn = base * np.exp(spread * noise) if base else spread * noise
        out[name] = jnp.asarray(drawn.astype(out[name].dtype))
    for name, factor in factors.items():
        out[name] = (out[name] * factor).astype(out[name].dtype)
    return out
```

```python
from contextlib import ExitStack

import concourse.bass as bass
from concourse import mybir

FP32 = mybir.dt.float32
BF16 = mybir.dt.bfloat16
ALU = mybir.AluOpType
ACT = mybir.ActivationFunctionType
AX = mybir.AxisListType

P = 128
BATCH, SEQ, D = 2, 2048, 256
H, DH = 16, 16
FF = 1024
KC = D // P
TOK = BATCH * SEQ
T = TOK // P
TPB = SEQ // P
GROUP = 512
NG = TOK // GROUP
SUB = GROUP // P
BANK = 512
CH = 1024
NCH = SEQ // CH
CPT = H * NCH
NBUF = 3
HALF = H // 2
EPS = 1e-5
BETA, THRESHOLD, STEPS = 0.9, 1.0, 5
PARTS = 3
Q_SLOTS = [0, 0, 0, 1, 1, 1, 2, 2]
K_SLOTS = [0, 1, 2, 0, 1, 2, 0, 1]
DRAIN = 3
LIF_OPS = 1 + 5 * (STEPS - 1)
N_PRELUDE_LOADS, N_WEIGHT_LOADS = 3, 10
PROD_AT = [8, 9, 11, 12, 13, 14, 16, 17], [22, 23, 25, 26, 27, 28, 30, 31]


def build(nc, x, w_in, b_in_col, b_in_row, w_out, b_out, wq, bq_col, wkv, bkv_row, temp, w_fc, w_proj, out):
    q_parts = nc.dram_tensor("q_parts", (PARTS, D, TOK), BF16).ap()
    k_parts = nc.dram_tensor("k_parts", (PARTS, D, TOK), BF16).ap()
    v_rows = nc.dram_tensor("v_rows", (TOK, D), FP32).ap()
    x2_rows = nc.dram_tensor("x2_rows", (TOK, D), FP32).ap()
    kb_parts = nc.dram_tensor("kb_parts", (PARTS, TOK, D), BF16).ap()
    vb_parts = nc.dram_tensor("vb_parts", (PARTS, TOK, D), BF16).ap()
    qb_cols = nc.dram_tensor("qb_cols", (T * P, D), FP32).ap()

    ctx = ExitStack()
    with ctx:
        def sb(name, shape, dt=FP32):
            return ctx.enter_context(nc.sbuf_tensor(name, shape, dt))

        def pb(name, shape):
            return ctx.enter_context(nc.psum_tensor(name, shape, FP32))

        def sem(name):
            return ctx.enter_context(nc.semaphore(name))

        big = sb("big", [P, H * SEQ])
        keys = big[:, :].bitcast(BF16).rearrange("p (b h m) -> p b h m", b=BATCH, h=H)
        expo = big[:, :].rearrange("p (t s) -> p t s", t=H)
        at = 0

        def carve(n):
            nonlocal at
            at += n
            return big[:, at - n:at]
        px = carve(SUB * D).rearrange("p (s d) -> p s d", s=SUB)
        pxn = carve(SUB * D).rearrange("p (s d) -> p s d", s=SUB)
        pxT = carve(KC * GROUP).rearrange("p (k n) -> p k n", k=KC)
        pqk = carve(2 * KC * GROUP).rearrange("p (m n) -> p m n", m=2 * KC)
        pres = carve(2 * KC * GROUP).rearrange("p (m n) -> p m n", m=2 * KC)
        pparts = carve(PARTS * KC * GROUP).bitcast(BF16).rearrange("p (a m n) -> p a m n", a=PARTS, m=2 * KC)
        pv_sb = carve(SUB * D).rearrange("p (s d) -> p s d", s=SUB)
        pstat = carve(SUB * 6).rearrange("p (s k) -> p s k", s=SUB)
        pmv = carve(SUB * 2).rearrange("p (s k) -> p s k", s=SUB)
        prstd = carve(SUB)
        pvar = carve(SUB)
        w_in_sb = carve(KC * 3 * D).rearrange("p (k n) -> p k n", k=KC)


        w_out_sb = sb("w_out_sb", [P, KC, D])
        wq_sb = sb("wq_sb", [P, KC, D])
        wkv_sb = sb("wkv_sb", [P, KC, 2 * D])
        w_fc_sb = sb("w_fc_sb", [P, KC, FF])
        w_proj_sb = sb("w_proj_sb", [P, FF // P, D])
        bin_col = sb("bin_col", [P, 2 * KC])
        bq_scaled = sb("bq_scaled", [P, KC])
        bqb_col = sb("bqb_col", [P, KC])
        temp_sb = sb("temp_sb", [P, T])
        ident = sb("ident", [P, P])
        ones = sb("ones", [1, P])
        power = sb("power", [P, SUB])

        shared = sb("shared", [P, 4 * SEQ // 2])
        qstack = shared[:, 0:2 * H * P // 2].bitcast(BF16).rearrange("p (r h n) -> p r h n", r=2, h=H)
        kvf = shared[:, 2048:2560]
        kvres = shared[:, 2560:3072]
        kvparts = shared[:, 3072:3840].bitcast(BF16).rearrange("p (a n) -> p a n", a=PARTS)
        bstack = shared[:, :].bitcast(BF16).rearrange("p (r a n) -> p r a n", r=2, a=2)
        shared2 = sb("shared2", [P, SEQ])
        xa = shared2[:, 0:512].rearrange("p (r d) -> p r d", r=2)
        va = shared2[:, 512:1024].rearrange("p (r d) -> p r d", r=2)
        opt = shared2[:, 1024:1280]
        optT = shared2[:, 1280:1536].rearrange("p (k n) -> p k n", k=KC)
        xn2 = shared2[:, 1536:1792]
        xn2T = shared2[:, 1792:2048].rearrange("p (k n) -> p k n", k=KC)
        prod = shared2[:, :]

        qcol = sb("qcol", [P, 2, D])
        pieces = sb("pieces", [P, 4, D])
        bv_row, bo_row = pieces[0:1, 0, :], pieces[0:1, 1, :]
        bkv = pieces[0:1, 2:4, :].rearrange("o a d -> o (a d)")
        x2_in = sb("x2_in", [P, D])
        qw = sb("qw", [P, NCH, HALF, 2 * DH])
        xin = sb("xin", [P, 2, D])
        xout = sb("xout", [P, 2, D])
        xn = sb("xn", [P, D])
        xnT = sb("xnT", [P, KC, P])
        hid = sb("hid", [P, FF])
        y = sb("y", [P, D])
        mem = sb("mem", [P, D])
        spk = sb("spk", [P, D])
        cnt = sb("cnt", [P, D])
        nmax = sb("nmax", [P, 2, H, NCH])
        esum = sb("esum", [P, 2, H, NCH])
        nrow = sb("nrow", [P, H])
        dlt = sb("dlt", [P, H, NCH])
        fac = sb("fac", [P, H, NCH])
        sume = sb("sume", [P, H, NCH])
        tot = sb("tot", [P, H])
        rec = sb("rec", [P, H])
        wgt = sb("wgt", [P, H, NCH])
        wsum = sb("wsum", [P, H])
        st = sb("st", [P, 2, 6])
        mv = sb("mv", [P, 2, 2])
        var = sb("var", [P, 2])
        rstd = sb("rstd", [P, 2])

        score = [pb(f"score{n}", [P, CH]) for n in range(NBUF)]
        bank_f = pb("bank_f", [P, BANK])
        bank_g = pb("bank_g", [P, BANK])

        w_in_loaded = sem("w_in_loaded")
        att_step, ffn_step, qkv_step, w_step = (sem(n) for n in ("att_step", "ffn_step", "qkv_step", "w_step"))
        w_loaded, consts, ident0, bq_ready = sem("w_loaded"), sem("consts"), sem("ident0"), sem("bq_ready")
        px_loaded, p_stats, p_aggr, p_rstd, p_xn = (sem(n) for n in ("px_loaded", "p_stats", "p_aggr", "p_rstd", "p_xn"))
        p_tr, p_xT, p_qk, p_qkf, p_v, p_vs = (sem(n) for n in ("p_tr", "p_xT", "p_qk", "p_qkf", "p_v", "p_vs"))
        p_split, p_stored = sem("p_split"), sem("p_stored")
        keys_loaded = [sem(f"keys_loaded{b}") for b in range(BATCH)]
        q_loaded = [sem(f"q_loaded{r}") for r in range(2)]
        xv_loaded = [sem(f"xv_loaded{r}") for r in range(2)]
        scores_a, max_a, exp_a = sem("scores_a"), sem("max_a"), sem("exp_a")
        att_min, att_dlt, att_fac, att_sum, att_rec, att_opt = (
            sem(n) for n in ("att_min", "att_dlt", "att_fac", "att_sum", "att_rec", "att_opt"))
        opt_tr, opt_T, oproj = sem("opt_tr"), sem("opt_T"), sem("oproj")
        ffn_x1 = sem("ffn_x1")
        ffn_stats, ffn_mv, ffn_xn, ffn_tr, ffn_xT = (sem(n) for n in ("ffn_stats", "ffn_mv", "ffn_xn", "ffn_tr", "ffn_xT"))
        ffn_fc, ffn_relu, ffn_sq, ffn_y, ffn_ysb = (sem(n) for n in ("ffn_fc", "ffn_relu", "ffn_sq", "ffn_y", "ffn_ysb"))
        lif, ffn_out = sem("lif"), sem("ffn_out")
        qkv_stats, qkv_mv, qkv_xn, qkv_tr, qkv_xT = (sem(n) for n in ("qkv_stats", "qkv_mv", "qkv_xn", "qkv_tr", "qkv_xT"))
        qkv_kv, qkv_kvf, qkv_q, qkv_qf, qkv_split = (sem(n) for n in ("qkv_kv", "qkv_kvf", "qkv_q", "qkv_qf", "qkv_split"))
        parts_stored = sem("parts_stored")
        x2_stored, qb_stored = ([sem(f"{n}{r}") for r in range(2)] for n in ("x2_stored", "qb_stored"))
        b_loaded = [sem(f"b_loaded{r}") for r in range(2)]
        x2_loaded = sem("x2_loaded")
        scores_b, max_b, exp_b = sem("scores_b"), sem("max_b"), sem("exp_b")
        w_min, w_dlt, w_fac, w_sum, w_rec, w_qw = (sem(n) for n in ("w_min", "w_dlt", "w_fac", "w_sum", "w_rec", "w_qw"))
        prod_ready, prod_kept, prod_added = sem("prod_ready"), sem("prod_kept"), sem("prod_added")
        pieces_loaded, x3_step, x3_ready = sem("pieces_loaded"), sem("x3_step"), sem("x3_ready")
        out_stored = [sem(f"out_stored{r}") for r in range(2)]

        block = ctx.enter_context(nc.Block())

        def need(eng, s, value):
            if not (isinstance(value, int) and value <= 0):
                eng.wait_ge(s, value)

        def stand_alone(eng, *waits):
            waits = [(s, n if isinstance(n, int) else eng.to_reg(n)) for s, n in waits]
            eng.wait_ge(consts, 4)
            for s, n in waits:
                need(eng, s, n)

        def tile_at(it, lag):
            if isinstance(it, int) and not 0 <= it - lag < T:
                return None
            return it - lag

        def iterations(eng, body, cuts=(T,)):
            for it in range(4):
                body(it, it % 2, 0)
            low = 4
            for n, cut in enumerate(cuts):
                with eng.Fori(low, cut, 2) as it:
                    body(it, 0, n)
                    body(it + 1, 1, n)
                low = cut
            for it in range(low, T + DRAIN):
                body(it, it % 2, len(cuts) - 1)

        def chunk_buffer(par, c):
            q, pair = CPT * par + c, 2 * CPT
            if q >= NBUF:
                return q % NBUF, NBUF
            return q, pair + q - max(n for n in range(pair) if n % NBUF == q)

        @block.sync
        def _(sp):
            loads = [
                (w_in_sb, w_in.rearrange("(k p) n -> p k n", p=P)),
                (bin_col[:, :], b_in_col),
                (bv_row, b_in_row),
                (w_out_sb[:, :, :], w_out.rearrange("(k p) n -> p k n", p=P)),
                (bo_row, b_out),
                (wq_sb[:, :, :], wq.rearrange("(k p) n -> p k n", p=P)),
                (bqb_col[:, :], bq_col),
                (wkv_sb[:, :, :], wkv.rearrange("(k p) n -> p k n", p=P)),
                (bkv, bkv_row),
                (temp_sb[:, 0:H], temp.broadcast_to([P, H])),
                (temp_sb[:, H:2 * H], temp.broadcast_to([P, H])),
                (w_fc_sb[:, :, :], w_fc.rearrange("(k p) n -> p k n", p=P)),
                (w_proj_sb[:, :, :], w_proj.rearrange("(k p) n -> p k n", p=P)),
            ]
            assert len(loads) == N_PRELUDE_LOADS + N_WEIGHT_LOADS

            def load_x(g):
                sp.dma_start(px, x[bass.ds(g * GROUP, GROUP), :].rearrange("(s p) d -> p s d", p=P)).then_inc(px_loaded, 16)

            def store_group(g):
                cols = bass.ds(g * GROUP, GROUP)
                stand_alone(sp, (p_vs, g + 1))
                sp.dma_start(v_rows[cols, :].rearrange("(s p) d -> p s d", p=P), pv_sb).then_inc(p_stored, 16)
                stand_alone(sp, (p_split, 4 * g + 4))
                for a in range(PARTS):
                    sp.dma_start(q_parts[a, :, cols].rearrange("(m p) n -> p m n", p=P), pparts[:, a, 0:KC, :]).then_inc(p_stored, 16)
                    sp.dma_start(k_parts[a, :, cols].rearrange("(m p) n -> p m n", p=P), pparts[:, a, KC:2 * KC, :]).then_inc(p_stored, 16)

            load_x(0)
            for n, (dst, src) in enumerate(loads):
                sp.dma_start(dst, src).then_inc(w_in_loaded if n < N_PRELUDE_LOADS else w_loaded, 16)
            with sp.Fori(0, NG - 1) as g:
                stand_alone(sp, (p_xn, g + 1))
                load_x(g + 1)
                store_group(g)
            store_group(NG - 1)

            sp.wait_ge(p_stored, 16 * 7 * NG)
            sp.wait_ge(p_qk, 4 * NG)
            sp.wait_ge(p_v, NG)

            def load_q(i, par):
                for s in range(8):
                    src = q_parts[Q_SLOTS[s], :, bass.ds(i * P, P)].rearrange("(h d) n -> d h n", d=DH)
                    sp.dma_start(qstack[s * DH:(s + 1) * DH, par, :, :], src).then_inc(q_loaded[par], 16)

            for b in range(BATCH):
                for s in range(8):
                    src = k_parts[K_SLOTS[s], :, b * SEQ:(b + 1) * SEQ].rearrange("(h d) m -> d h m", d=DH)
                    sp.dma_start(keys[s * DH:(s + 1) * DH, b, :, :], src).then_inc(keys_loaded[b], 16)
                if b == 0:
                    load_q(0, 0)

            def phase_a(it, par, _):
                i = tile_at(it, 0)
                if i is not None:
                    if not (isinstance(i, int) and i == T - 1):
                        stand_alone(sp, (scores_a, CPT * i))
                        load_q(i + 1, 1 - par)
                    stand_alone(sp, (att_opt, i - 1), (ffn_x1, i - 1))
                    sp.dma_start(xa[:, par, :], x[bass.ds(i * P, P), :]).then_inc(xv_loaded[par], 16)
                    sp.dma_start(va[:, par, :], v_rows[bass.ds(i * P, P), :]).then_inc(xv_loaded[par], 16)
                i = tile_at(it, 3)
                if i is not None:
                    r = (par + 1) % 2
                    row = bass.ds(i * P, P)
                    stand_alone(sp, (ffn_out, i + 1))
                    sp.dma_start(x2_rows[row, :], xout[:, r, :]).then_inc(x2_stored[r], 16)
                    stand_alone(sp, (qkv_qf, i + 1))
                    sp.dma_start(qb_cols[row, :], qcol[:, r, :]).then_inc(qb_stored[r], 16)
                    stand_alone(sp, (qkv_split, 4 * i + 4))
                    for a in range(PARTS):
                        sp.dma_start(kb_parts[a, row, :], kvparts[:, a, 0:D]).then_inc(parts_stored, 16)
                        sp.dma_start(vb_parts[a, row, :], kvparts[:, a, D:2 * D]).then_inc(parts_stored, 16)
            iterations(sp, phase_a, (T - 2,))

            for r in range(2):
                sp.wait_ge(x2_stored[r], 16 * T // 2)
                sp.wait_ge(qb_stored[r], 16 * T // 2)
            sp.wait_ge(parts_stored, 16 * 2 * PARTS * T)

            def load_b(i, par):
                for s in range(8):
                    for side, (parts, slots) in enumerate(((kb_parts, Q_SLOTS), (vb_parts, K_SLOTS))):
                        src = parts[slots[s], bass.ds(i * P, P), :].rearrange("(r j) d -> r (j d)", r=DH)
                        sp.dma_start(bstack[s * DH:(s + 1) * DH, par, side, :], src).then_inc(b_loaded[par], 16)
                sp.dma_start(qcol[:, par, :], qb_cols[bass.ds(i * P, P), :]).then_inc(b_loaded[par], 16)
            sp.wait_ge(scores_a, CPT * T)
            load_b(0, 0)

            def phase_b(it, par, _):
                i = tile_at(it, 0)
                if i is not None and not (isinstance(i, int) and i == T - 1):
                    stand_alone(sp, (scores_b, CPT * i), (w_qw, 2 * i))
                    load_b(i + 1, 1 - par)
                i = tile_at(it, 1)
                if i is not None:
                    stand_alone(sp, (x3_ready, i))
                    sp.dma_start(x2_in[:, :], x2_rows[bass.ds(i * P, P), :]).then_inc(x2_loaded, 16)
                    stand_alone(sp, (prod_added, 4 * i + 4))
                    for g in range(4):
                        sp.dma_start(pieces[:, g, :], prod[32 * g:32 * g + DH, :].rearrange("r (j d) -> r j d", j=8)) \
                          .then_inc(pieces_loaded, 16)
                i = tile_at(it, 3)
                if i is not None:
                    r = (par + 1) % 2
                    stand_alone(sp, (ffn_out, T + i + 1))
                    sp.dma_start(out[bass.ds(i * P, P), :], xout[:, r, :]).then_inc(out_stored[r], 16)
            iterations(sp, phase_b, (T - 2,))
            for r in range(2):
                sp.wait_ge(out_stored[r], 16 * T // 2)

        @block.tensor
        def _(pe):
            mm = nc.tensor.matmul

            def transpose2(dst, src):
                for k in range(KC):
                    last = nc.tensor.transpose(dst[:, k * P:(k + 1) * P], src[:, k * P:(k + 1) * P], ident[:, :])
                return last

            pe.wait_ge(w_in_loaded, 16 * N_PRELUDE_LOADS)
            pe.wait_ge(consts, 4)

            def tr(g):
                pe.wait_ge(p_xn, g + 1)
                need(pe, p_xT, g)
                for k in range(KC):
                    for s in range(SUB):
                        last = nc.tensor.transpose(score[0][:, k * GROUP + s * P:k * GROUP + (s + 1) * P],
                                                   pxn[:, s, k * P:(k + 1) * P], ident[:, :])
                last.then_inc(p_tr, 1)

            def project(g):
                pe.wait_ge(p_xT, g + 1)
                need(pe, p_qkf, g)
                for m in range(2 * KC):
                    dst = score[1 + m // 2][:, (m % 2) * GROUP:(m % 2 + 1) * GROUP]
                    for k in range(KC):
                        last = mm(dst, w_in_sb[:, k, m * P:(m + 1) * P], pxT[:, k, :], start=(k == 0), stop=(k == KC - 1))
                    last.then_inc(p_qk, 1)
                need(pe, p_vs, g)
                for s in range(SUB):
                    dst = (bank_f, bank_g)[s // 2][:, (s % 2) * D:(s % 2 + 1) * D]
                    for k in range(KC):
                        mm(dst, pxT[:, k, s * P:(s + 1) * P], w_in_sb[:, k, 2 * D:3 * D], start=(k == 0), stop=False)
                    last = mm(dst, ones[:, :], bv_row, start=False, stop=True)
                last.then_inc(p_v, 1)
            tr(0)
            tr(1)
            project(0)
            with pe.Fori(1, NG - 1) as g:
                tr(g + 1)
                project(g)
            project(NG - 1)
            pe.wait_ge(p_qkf, NG)
            pe.wait_ge(p_vs, NG)
            pe.wait_ge(w_loaded, 16 * N_WEIGHT_LOADS)

            def ffn_transpose(n):
                pe.wait_ge(ffn_xn, n + 1)
                need(pe, ffn_ysb, n)
                transpose2(bank_f, xn).then_inc(ffn_tr, 1)

            def ffn_up(n, f, part):
                if f % 4 == 0:
                    if part == 0:
                        pe.wait_ge(ffn_xT, n + 1)
                    else:
                        pe.wait_ge(ffn_relu, 2 * n + 1)
                for k in range(KC):
                    last = mm(bank_f[:, (f % 4) * P:(f % 4 + 1) * P], w_fc_sb[:, k, f * P:(f + 1) * P], xnT[:, k, :],
                              start=(k == 0), stop=(k == KC - 1))
                if f % 4 == 3:
                    last.then_inc(ffn_fc, 1)

            def ffn_down(n, f):
                if f == 0:
                    pe.wait_ge(ffn_sq, 2 * n + 2)
                last = mm(bank_f[:, 0:D], hid[:, f * P:(f + 1) * P], w_proj_sb[:, f, :], start=(f == 0), stop=(f == FF // P - 1))
                if f == FF // P - 1:
                    last.then_inc(ffn_y, 1)

            def phase_a(it, par, b):
                i, i1, i3 = tile_at(it, 0), tile_at(it, 1), tile_at(it, 3)
                if isinstance(it, int):
                    b = min(it, T - 1) // TPB
                if i is not None:
                    if isinstance(i, int):
                        pe.wait_ge(q_loaded[par], 128 * (i // 2 + 1))
                    else:
                        pe.wait_ge(q_loaded[par], 64 * (i - par) + 128)
                    pe.wait_ge(keys_loaded[b], 128)
                for c in range(CPT):
                    if i is not None:
                        buf, ago = chunk_buffer(par, c)
                        need(pe, exp_a, CPT * i + c - ago + 1)
                        for k in range(CH // BANK):
                            col = (c % NCH) * CH + k * BANK
                            last = mm(score[buf][:, k * BANK:(k + 1) * BANK], qstack[:, par, c // NCH, :],
                                      keys[:, b, c // NCH, col:col + BANK], start=True, stop=True)
                        last.then_inc(scores_a, 1)
                    if i3 is not None:
                        if c == 12:
                            pe.wait_ge(qkv_xn, i3 + 1)
                            need(pe, qkv_qf, i3)
                            if i1 is not None:
                                pe.wait_ge(ffn_x1, i1 + 1)
                            transpose2(bank_g, xn2).then_inc(qkv_tr, 1)
                        if c == 15:
                            pe.wait_ge(qkv_xT, i3 + 1)
                            for k in range(KC):
                                mm(bank_g[:, :], xn2T[:, k, :], wkv_sb[:, k, :], start=(k == 0), stop=False)
                            mm(bank_g[:, :], ones[:, :], bkv, start=False, stop=True).then_inc(qkv_kv, 1)
                        if c == 20:
                            pe.wait_ge(qkv_kvf, i3 + 1)
                            for m in range(KC):
                                for k in range(KC):
                                    last = mm(bank_g[:, m * P:(m + 1) * P], wq_sb[:, k, m * P:(m + 1) * P], xn2T[:, k, :],
                                              start=(k == 0), stop=(k == KC - 1))
                            last.then_inc(qkv_q, 1)
                    if i1 is not None:
                        if c == 7:
                            pe.wait_ge(att_opt, i1 + 1)
                            need(pe, ffn_x1, i1)
                            need(pe, qkv_qf, it - DRAIN)
                            transpose2(bank_g, opt).then_inc(opt_tr, 1)
                        if c == 10:
                            pe.wait_ge(opt_T, i1 + 1)
                            for k in range(KC):
                                mm(bank_g[:, 0:D], optT[:, k, :], w_out_sb[:, k, :], start=(k == 0), stop=False)
                            mm(bank_g[:, 0:D], ones[:, :], bo_row, start=False, stop=True).then_inc(oproj, 1)
                        if c == 16:
                            ffn_transpose(i1)
                        if c in (18, 19, 21, 22):
                            f = 2 * (18, 19, 21, 22).index(c)
                            ffn_up(i1, f, f // 4)
                            ffn_up(i1, f + 1, f // 4)
                        if 26 <= c < 30:
                            ffn_down(i1, 2 * (c - 26))
                            ffn_down(i1, 2 * (c - 26) + 1)
            iterations(pe, phase_a, (TPB, T))

            def product(i, half, sc, rr):
                if rr == 0:
                    if sc == 0:
                        pe.wait_ge(w_qw, 2 * i + half + 1)
                    if half == 0:
                        need(pe, prod_kept, 4 * i + sc)
                        if sc == 0:
                            need(pe, prod_added, 4 * i)
                            if isinstance(i, int) and i == 0:
                                pe.wait_ge(qkv_qf, T)
                    else:
                        pe.wait_ge(prod_kept, 4 * i + 4)
                        need(pe, prod_added, 4 * i + sc)
                for g in range(4):
                    n = 4 * rr + g
                    last = mm(bank_g[32 * g:32 * g + 32, :], qw[:, sc * BANK // CH, n, :],
                              expo[:, HALF * half + n, sc * BANK:(sc + 1) * BANK], start=(rr == 0), stop=(rr == 1))
                if rr == 1:
                    last.then_inc(prod_ready, 1)

            def phase_b(it, par, _):
                i, i1, i2 = tile_at(it, 0), tile_at(it, 1), tile_at(it, 2)
                if i is not None:
                    if isinstance(i, int):
                        pe.wait_ge(b_loaded[par], 16 * 17 * (i // 2 + 1))
                    else:
                        pe.wait_ge(b_loaded[par], 8 * 17 * (i - par) + 16 * 17)
                for c in range(CPT):
                    if i is not None:
                        buf, ago = chunk_buffer(par, c)
                        if isinstance(i, int) and i == 0 and c < NBUF:
                            pe.wait_ge(exp_a, CPT * T)
                        need(pe, exp_b, CPT * i + c - ago + 1)
                        row = c // NCH * P
                        for k in range(CH // BANK):
                            col = (c % NCH) * CH + k * BANK
                            last = mm(score[buf][:, k * BANK:(k + 1) * BANK], bstack[:, par, 0, row:row + P],
                                      bstack[:, par, 1, col:col + BANK], start=True, stop=True)
                        last.then_inc(scores_b, 1)
                    if i2 is not None:
                        if c == 2:
                            ffn_transpose(T + i2)
                        if c in (3, 4, 6, 7):
                            f = 2 * (3, 4, 6, 7).index(c)
                            ffn_up(T + i2, f, f // 4)
                            ffn_up(T + i2, f + 1, f // 4)
                        if 18 <= c < 22:
                            ffn_down(T + i2, 2 * (c - 18))
                            ffn_down(T + i2, 2 * (c - 18) + 1)
                    if i1 is not None and c in PROD_AT[0]:
                        n = PROD_AT[0].index(c)
                        product(i1, 1, n // 2, n % 2)
                    if i is not None and c in PROD_AT[1]:
                        n = PROD_AT[1].index(c)
                        product(i, 0, n // 2, n % 2)
            iterations(pe, phase_b)

        @block.vector
        def _(dve):
            v = nc.vector
            v.memset(ones[:, :], 1.0).then_inc(consts, 1)
            v.memset(power[:, :], -0.5).then_inc(consts, 1)
            v.memset(qw[:, :, :, :], 0.0).then_inc(consts, 1)
            dve.wait_ge(w_in_loaded, 16 * N_PRELUDE_LOADS)
            v.tensor_scalar(bq_scaled[:, :], bin_col[:, 0:KC], DH ** -0.5, None, ALU.mult).then_inc(bq_ready, 1)

            def norm(g):
                dve.wait_ge(px_loaded, 16 * (g + 1))
                for s in range(SUB):
                    v.bn_stats(pstat[:, s, :], px[:, s, :]).then_inc(p_stats, 1)
                need(dve, p_rstd, 2 * g)
                for s in range(SUB):
                    stand_alone(dve, (p_stats, SUB * g + s + 1))
                    v.bn_aggr(pmv[:, s, :], pstat[:, s, :]).then_inc(p_aggr, 1)
                dve.wait_ge(p_rstd, 2 * g + 2)
                need(dve, p_tr, g)
                dve.wait_ge(p_aggr, SUB * g + SUB)
                for s in range(SUB):
                    last = v.tensor_scalar(pxn[:, s, :], px[:, s, :], pmv[:, s, 0:1], prstd[:, s:s + 1], ALU.subtract, ALU.mult)
                last.then_inc(p_xn, 1)

            def split(g):
                dve.wait_ge(p_qkf, g + 1)
                need(dve, p_stored, 16 * 7 * g)
                v.tensor_copy(pparts[:, 0, :, :], pqk).then_inc(p_split, 1)
                dve.wait_ge(p_split, 4 * g + 1)
                v.tensor_tensor(pres, pqk, pparts[:, 0, :, :], ALU.subtract).then_inc(p_split, 1)
                dve.wait_ge(p_split, 4 * g + 2)
                v.tensor_copy(pparts[:, 1, :, :], pres).then_inc(p_split, 1)
                dve.wait_ge(p_split, 4 * g + 3)
                v.tensor_tensor(pparts[:, 2, :, :], pres, pparts[:, 1, :, :], ALU.subtract).then_inc(p_split, 1)
            norm(0)
            norm(1)
            split(0)
            with dve.Fori(1, NG - 1) as g:
                norm(g + 1)
                split(g)
            split(NG - 1)

            def ffn_norm(n, par, done, count):
                dve.wait_ge(done, count)
                v.bn_stats(st[:, 0, :], xin[:, par, :]).then_inc(ffn_stats, 1)
                stand_alone(dve, (ffn_stats, n + 1), (ffn_xn, n))
                v.bn_aggr(mv[:, 0, :], st[:, 0, :]).then_inc(ffn_mv, 1)

            def ffn_result(n, par, stored, count):
                dve.wait_ge(lif, LIF_OPS * (n + 1))
                need(dve, stored, count)
                v.scalar_tensor_tensor(out=xout[:, par, :], in0=cnt[:, :], scalar=1.0 / STEPS, in1=xin[:, par, :],
                                       op0=ALU.mult, op1=ALU.add).then_inc(ffn_out, 1)

            def phase_a(it, par, _):
                i, i1, i2, i3 = (tile_at(it, n) for n in range(4))
                r1, r3 = 1 - par, 1 - par
                for c in range(CPT):
                    if i is not None:
                        if c == 0:
                            need(dve, att_dlt, i - 1)
                        dve.wait_ge(scores_a, CPT * i + c + 1)
                        v.tensor_reduce(nmax[:, par, c // NCH, c % NCH:c % NCH + 1], score[chunk_buffer(par, c)[0]][:, :],
                                        AX.X, ALU.max, negate=True).then_inc(max_a, 1)
                    if i1 is not None:
                        if c == 0:
                            dve.wait_ge(max_a, CPT * i1 + CPT)
                            need(dve, att_dlt, i1)
                            v.tensor_tensor(nrow[:, :], nmax[:, r1, :, 0], nmax[:, r1, :, 1], ALU.min).then_inc(att_min, 1)
                        if c == 4:
                            dve.wait_ge(att_sum, 2 * i1 + 2)
                            v.reciprocal(rec[:, :], tot[:, :]).then_inc(att_rec, 1)
                        if c == 11:
                            dve.wait_ge(oproj, i1 + 1)
                            need(dve, ffn_out, i1 - 1)
                            if isinstance(i1, int):
                                dve.wait_ge(xv_loaded[r1], 32 * (i1 // 2 + 1))
                            else:
                                dve.wait_ge(xv_loaded[r1], 16 * (i1 - r1) + 32)
                            v.tensor_tensor(xin[:, r1, :], bank_g[:, 0:D], xa[:, r1, :], ALU.add).then_inc(ffn_x1, 1)
                        if c == 12:
                            ffn_norm(i1, r1, ffn_x1, i1 + 1)
                    if i3 is not None and c == 5:
                        dve.wait_ge(ffn_out, i3 + 1)
                        v.bn_stats(st[:, 1, :], xout[:, r3, :]).then_inc(qkv_stats, 1)
                        stand_alone(dve, (qkv_stats, i3 + 1), (qkv_xn, i3))
                        v.bn_aggr(mv[:, 1, :], st[:, 1, :]).then_inc(qkv_mv, 1)
                    if i2 is not None and c == 24:
                        need(dve, qkv_xn, i2 - 1)
                        ffn_result(i2, par, x2_stored[par], 8 * (i2 - par))
            iterations(dve, phase_a)

            def row_min(i, par, half):
                t0 = HALF * half
                dve.wait_ge(max_b, CPT * i + CPT // 2 * (half + 1))
                need(dve, w_dlt, 2 * i + half)
                v.tensor_tensor(nrow[:, 0:HALF], nmax[:, par, t0:t0 + HALF, 0], nmax[:, par, t0:t0 + HALF, 1], ALU.min) \
                    .then_inc(w_min, 1)

            def row_rec(i, half):
                dve.wait_ge(w_sum, 2 * (2 * i + half) + 2)
                v.reciprocal(rec[:, 0:HALF], tot[:, 0:HALF]).then_inc(w_rec, 1)

            def phase_b(it, par, _):
                i, i1, i2, i3 = (tile_at(it, n) for n in range(4))
                for c in range(CPT):
                    if i is not None:
                        if c == 0:
                            need(dve, w_dlt, 2 * (i - 1))
                            if isinstance(i, int) and i == 0:
                                dve.wait_ge(att_dlt, T)
                        dve.wait_ge(scores_b, CPT * i + c + 1)
                        v.tensor_reduce(nmax[:, par, c // NCH, c % NCH:c % NCH + 1], score[chunk_buffer(par, c)[0]][:, :],
                                        AX.X, ALU.max, negate=True).then_inc(max_b, 1)
                    if i1 is not None:
                        if c == 0:
                            row_min(i1, 1 - par, 1)
                        if c == 4:
                            row_rec(i1, 1)
                        for sc in range(4):
                            if c == PROD_AT[0][2 * sc + 1] + 1:
                                dve.wait_ge(prod_ready, 8 * i1 + 4 + sc + 1)
                                dve.wait_ge(prod_kept, 4 * i1 + sc + 1)
                                cols = prod[:, sc * BANK:(sc + 1) * BANK]
                                v.tensor_tensor(cols, bank_g[:, :], cols, ALU.add).then_inc(prod_added, 1)
                        if c == CPT - 1:
                            ffn_norm(T + i1, 1 - par, x3_ready, i1 + 1)
                    if i is not None:
                        if c == 16:
                            row_min(i, par, 0)
                        if c == 20:
                            row_rec(i, 0)
                    if i3 is not None and c == 26:
                        if isinstance(i3, int) and i3 < 2:
                            dve.wait_ge(x2_stored[1 - par], 16 * T // 2)
                            dve.wait_ge(qkv_xn, T)
                        ffn_result(T + i3, 1 - par, out_stored[1 - par], 8 * (i3 - (1 - par)))
            iterations(dve, phase_b)

        @block.scalar
        def _(act):
            a = nc.scalar
            act.wait_ge(bq_ready, 1)
            act.wait_ge(w_in_loaded, 16 * N_PRELUDE_LOADS)

            def group(g):
                act.wait_ge(p_tr, g + 1)
                need(act, p_v, g)
                for k in range(KC):
                    last = a.activation(pxT[:, k, :], score[0][:, k * GROUP:(k + 1) * GROUP], ACT.Copy)
                last.then_inc(p_xT, 1)
                need(act, p_split, 4 * g)
                for m in range(2 * KC):
                    act.wait_ge(p_qk, 4 * g + m + 1)
                    src = score[1 + m // 2][:, (m % 2) * GROUP:(m % 2 + 1) * GROUP]
                    if m < KC:
                        last = a.activation(pqk[:, m, :], src, ACT.Identity, bias=bq_scaled[:, m:m + 1], scale=DH ** -0.5)
                    else:
                        last = a.activation(pqk[:, m, :], src, ACT.Identity, bias=bin_col[:, m:m + 1])
                last.then_inc(p_qkf, 1)
                act.wait_ge(p_v, g + 1)
                need(act, p_stored, 16 * 7 * g)
                a.activation(pv_sb[:, 0:2, :], bank_f[:, :].rearrange("p (s d) -> p s d", s=2), ACT.Copy)
                a.activation(pv_sb[:, 2:4, :], bank_g[:, :].rearrange("p (s d) -> p s d", s=2), ACT.Copy).then_inc(p_vs, 1)
            group(0)
            with act.Fori(1, NG) as g:
                group(g)

            def ffn_columns(n):
                act.wait_ge(ffn_tr, n + 1)
                need(act, ffn_fc, 2 * n)
                a.activation(xnT[:, :, :], bank_f[:, 0:D].rearrange("p (k n) -> p k n", k=KC), ACT.Copy).then_inc(ffn_xT, 1)

            def ffn_act(n, part):
                act.wait_ge(ffn_fc, 2 * n + part + 1)
                if part == 0:
                    need(act, ffn_y, n)
                a.activation(hid[:, part * BANK:(part + 1) * BANK], bank_f[:, :], ACT.Relu).then_inc(ffn_relu, 1)

            def ffn_take(n):
                act.wait_ge(ffn_y, n + 1)
                need(act, lif, LIF_OPS * n)
                a.activation(y[:, :], bank_f[:, 0:D], ACT.Copy).then_inc(ffn_ysb, 1)

            act.wait_ge(w_loaded, 16 * N_WEIGHT_LOADS)

            def phase_a(it, par, _):
                i, i1, i3 = tile_at(it, 0), tile_at(it, 1), tile_at(it, 3)
                for c in range(CPT):
                    if i is not None:
                        if c == 0:
                            need(act, att_sum, 2 * (i - 1))
                        act.wait_ge(max_a, CPT * i + c + 1)
                        s = score[chunk_buffer(par, c)[0]]
                        a.activation(s[:, :], s[:, :], ACT.Exp, bias=nmax[:, par, c // NCH, c % NCH:c % NCH + 1],
                                     accum_out=esum[:, par, c // NCH, c % NCH:c % NCH + 1]).then_inc(exp_a, 1)
                    if i1 is not None:
                        if c == 2:
                            act.wait_ge(att_dlt, i1 + 1)
                            need(act, att_sum, 2 * i1)
                            a.activation(fac[:, :, :], dlt[:, :, :], ACT.Exp).then_inc(att_fac, 1)
                        if c == 7:
                            act.wait_ge(opt_tr, i1 + 1)
                            a.activation(optT[:, :, :], bank_g[:, 0:D].rearrange("p (k n) -> p k n", k=KC), ACT.Copy) \
                                .then_inc(opt_T, 1)
                        if c == 16:
                            ffn_columns(i1)
                        if c == 19:
                            ffn_act(i1, 0)
                        if c == 22:
                            ffn_act(i1, 1)
                        if c == 30:
                            ffn_take(i1)
                    if i3 is not None:
                        r = 1 - par
                        if c == 13:
                            act.wait_ge(qkv_tr, i3 + 1)
                            need(act, qkv_q, i3)
                            a.activation(xn2T[:, :, :], bank_g[:, 0:D].rearrange("p (k n) -> p k n", k=KC), ACT.Copy) \
                                .then_inc(qkv_xT, 1)
                        if c == 16:
                            act.wait_ge(qkv_kv, i3 + 1)
                            need(act, qkv_split, 4 * i3)
                            a.activation(kvf[:, 0:D], bank_g[:, 0:D], ACT.Copy, scale=temp_sb[:, bass.ds(i3, 1)])
                            a.activation(kvf[:, D:2 * D], bank_g[:, D:2 * D], ACT.Copy).then_inc(qkv_kvf, 1)
                        if c == 21:
                            act.wait_ge(qkv_q, i3 + 1)
                            need(act, qb_stored[r], 8 * (i3 - r))
                            for m in range(KC):
                                last = a.activation(qcol[:, r, m * P:(m + 1) * P], bank_g[:, m * P:(m + 1) * P], ACT.Identity,
                                                    bias=bqb_col[:, m:m + 1])
                            last.then_inc(qkv_qf, 1)
            iterations(act, phase_a)

            def row_fac(i, half):
                act.wait_ge(w_dlt, 2 * i + half + 1)
                need(act, w_qw, 2 * i + half)
                a.activation(fac[:, 0:HALF, :], dlt[:, 0:HALF, :], ACT.Exp).then_inc(w_fac, 1)

            def phase_b(it, par, _):
                i, i1, i2 = tile_at(it, 0), tile_at(it, 1), tile_at(it, 2)
                for c in range(CPT):
                    if i is not None:
                        if c == 0:
                            need(act, w_sum, 2 * 2 * (i - 1))
                            if isinstance(i, int) and i == 0:
                                act.wait_ge(att_sum, 2 * T)
                            need(act, prod_ready, 8 * (i - 1) + 4)
                        if c == CPT // 2:
                            need(act, prod_ready, 8 * i)
                        act.wait_ge(max_b, CPT * i + c + 1)
                        a.activation(expo[:, c // NCH, (c % NCH) * CH:(c % NCH + 1) * CH], score[chunk_buffer(par, c)[0]][:, :],
                                     ACT.Exp, bias=nmax[:, par, c // NCH, c % NCH:c % NCH + 1],
                                     accum_out=esum[:, par, c // NCH, c % NCH:c % NCH + 1]).then_inc(exp_b, 1)
                    if i1 is not None and c == 2:
                        row_fac(i1, 1)
                    if i2 is not None:
                        if c == 2:
                            ffn_columns(T + i2)
                        if c == 5:
                            ffn_act(T + i2, 0)
                        if c == 8:
                            ffn_act(T + i2, 1)
                        if c == 27:
                            ffn_take(T + i2)
                    if i is not None:
                        if c == 17:
                            row_fac(i, 0)
                        for sc in range(4):
                            if c == min(PROD_AT[1][2 * sc + 1] + 1, CPT - 1):
                                act.wait_ge(prod_ready, 8 * i + sc + 1)
                                need(act, pieces_loaded, 16 * 4 * i)
                                a.activation(prod[:, sc * BANK:(sc + 1) * BANK], bank_g[:, :], ACT.Copy).then_inc(prod_kept, 1)
            iterations(act, phase_b)

        @block.gpsimd
        def _(pool):
            g_ = nc.gpsimd
            g_.memset(ident[:, :], 0.0).then_inc(ident0, 1)
            pool.wait_ge(ident0, 1)
            g_.affine_select(out=ident[:, :], in_=ident[:, :], compare_op=ALU.not_equal, fill=1.0, base=0,
                             pattern=[[-1, P]], channel_multiplier=1).then_inc(consts, 1)
            pool.wait_ge(consts, 4)

            def group_rstd(g):
                stand_alone(pool, (p_aggr, SUB * g + SUB), (p_xn, g))
                g_.tensor_scalar(pvar, pmv[:, :, 1], EPS, 0.0, ALU.add, ALU.add).then_inc(p_rstd, 1)
                pool.wait_ge(p_rstd, 2 * g + 1)
                g_.tensor_tensor(prstd, pvar, power[:, 0:SUB], ALU.pow).then_inc(p_rstd, 1)
            group_rstd(0)
            with pool.Fori(1, NG) as g:
                group_rstd(g)

            def normalise(n, which, got, step, dst, src, free, count):
                stand_alone(pool, (got, n + 1))
                g_.tensor_scalar(var[:, which:which + 1], mv[:, which, 1:2], EPS, 0.0, ALU.add, ALU.add).then_inc(step, 1)
                pool.wait_ge(step, 2 * n + 1)
                g_.tensor_tensor(rstd[:, which:which + 1], var[:, which:which + 1], power[:, 0:1], ALU.pow).then_inc(step, 1)
                stand_alone(pool, (step, 2 * n + 2), (free, count))
                return g_.tensor_scalar(dst, src, mv[:, which, 0:1], rstd[:, which:which + 1], ALU.subtract, ALU.mult)

            def square(n, part):
                pool.wait_ge(ffn_relu, 2 * n + part + 1)
                h = hid[:, part * BANK:(part + 1) * BANK]
                g_.tensor_tensor(h, h, h, ALU.mult).then_inc(ffn_sq, 1)

            def neuron(n, steps):
                def op(k, ins):
                    ins.then_inc(lif, 1)
                    stand_alone(pool, (lif, LIF_OPS * n + k))
                for step in steps:
                    k = 5 * (step - 2) + 1
                    if step == 1:
                        stand_alone(pool, (ffn_ysb, n + 1), (ffn_out, n))
                        op(1, g_.tensor_scalar(cnt[:, :], y[:, :], THRESHOLD, 0.0, ALU.is_gt, ALU.add))
                        continue
                    last_mem, last_spk = (y, cnt) if step == 2 else (mem, spk)
                    op(k + 1, g_.tensor_scalar(mem[:, :], last_mem[:, :], BETA, 0.0, ALU.mult, ALU.add))
                    op(k + 2, g_.tensor_tensor(mem[:, :], mem[:, :], y[:, :], ALU.add))
                    op(k + 3, g_.tensor_tensor(mem[:, :], mem[:, :], last_spk[:, :], ALU.subtract))
                    op(k + 4, g_.tensor_scalar(spk[:, :], mem[:, :], THRESHOLD, 0.0, ALU.is_gt, ALU.add))
                    op(k + 5, g_.tensor_tensor(cnt[:, :], cnt[:, :], spk[:, :], ALU.add))

            def spread(ap, m):
                return ap.unsqueeze(2).broadcast_to([P, ap.shape[1], m])

            def normalise_rows(i, par):
                pool.wait_ge(att_min, i + 1)
                g_.tensor_tensor(dlt[:, :, :], spread(nrow[:, :], NCH), nmax[:, par, :, :], ALU.subtract).then_inc(att_dlt, 1)
                pool.wait_ge(att_fac, i + 1)
                pool.wait_ge(exp_a, CPT * i + CPT)
                g_.tensor_tensor(sume[:, :, :], esum[:, par, :, :], fac[:, :, :], ALU.mult).then_inc(att_sum, 1)
                pool.wait_ge(att_sum, 2 * i + 1)
                g_.tensor_tensor(tot[:, :], sume[:, :, 0], sume[:, :, 1], ALU.add).then_inc(att_sum, 1)
                pool.wait_ge(att_rec, i + 1)
                g_.tensor_tensor(wgt[:, :, :], sume[:, :, :], spread(rec[:, :], NCH), ALU.mult).then_inc(att_step, 1)
                pool.wait_ge(att_step, 2 * i + 1)
                g_.tensor_tensor(wsum[:, :], wgt[:, :, 0], wgt[:, :, 1], ALU.add).then_inc(att_step, 1)
                pool.wait_ge(att_step, 2 * i + 2)
                if isinstance(i, int):
                    pool.wait_ge(xv_loaded[par], 32 * (i // 2 + 1))
                else:
                    pool.wait_ge(xv_loaded[par], 16 * (i - par) + 32)
                need(pool, opt_tr, i)
                g_.tensor_tensor(opt.rearrange("p (h d) -> p h d", h=H), va[:, par, :].rearrange("p (h d) -> p h d", h=H),
                                 spread(wsum[:, :], DH), ALU.mult).then_inc(att_opt, 1)

            def split_kv(i):
                stand_alone(pool, (qkv_kvf, i + 1), (parts_stored, 16 * 2 * PARTS * i))
                g_.tensor_scalar(kvparts[:, 0, :], kvf, 1.0, 0.0, ALU.mult, ALU.add).then_inc(qkv_split, 1)
                pool.wait_ge(qkv_split, 4 * i + 1)
                g_.tensor_tensor(kvres, kvf, kvparts[:, 0, :], ALU.subtract).then_inc(qkv_split, 1)
                stand_alone(pool, (qkv_split, 4 * i + 2))
                g_.tensor_scalar(kvparts[:, 1, :], kvres, 1.0, 0.0, ALU.mult, ALU.add).then_inc(qkv_split, 1)
                pool.wait_ge(qkv_split, 4 * i + 3)
                g_.tensor_tensor(kvparts[:, 2, :], kvres, kvparts[:, 1, :], ALU.subtract).then_inc(qkv_split, 1)

            def phase_a(it, par, _):
                i1, i2, i3 = (tile_at(it, n) for n in (1, 2, 3))
                if i1 is not None:
                    normalise_rows(i1, 1 - par)
                if i3 is not None:
                    normalise(i3, 1, qkv_mv, qkv_step, xn2, xout[:, 1 - par, :], qkv_tr, i3).then_inc(qkv_xn, 1)
                if i2 is not None:
                    neuron(i2, (1, 2))
                if i1 is not None:
                    normalise(i1, 0, ffn_mv, ffn_step, xn[:, :], xin[:, 1 - par, :], ffn_tr, i1).then_inc(ffn_xn, 1)
                if i2 is not None:
                    neuron(i2, (3, 4, 5))
                if i1 is not None:
                    square(i1, 0)
                    square(i1, 1)
                if i3 is not None:
                    split_kv(i3)
            iterations(pool, phase_a)

            def weigh_q(i, par, half):
                n = 2 * i + half
                t0 = HALF * half
                pool.wait_ge(w_min, n + 1)
                g_.tensor_tensor(dlt[:, 0:HALF, :], spread(nrow[:, 0:HALF], NCH), nmax[:, par, t0:t0 + HALF, :], ALU.subtract) \
                    .then_inc(w_dlt, 1)
                pool.wait_ge(w_fac, n + 1)
                pool.wait_ge(exp_b, CPT * i + CPT // 2 * (half + 1))
                g_.tensor_tensor(sume[:, 0:HALF, :], esum[:, par, t0:t0 + HALF, :], fac[:, 0:HALF, :], ALU.mult).then_inc(w_sum, 1)
                pool.wait_ge(w_sum, 2 * n + 1)
                g_.tensor_tensor(tot[:, 0:HALF], sume[:, 0:HALF, 0], sume[:, 0:HALF, 1], ALU.add).then_inc(w_sum, 1)
                pool.wait_ge(w_rec, n + 1)
                g_.tensor_tensor(wgt[:, 0:HALF, :], fac[:, 0:HALF, :], spread(rec[:, 0:HALF], NCH), ALU.mult).then_inc(w_step, 1)
                pool.wait_ge(w_step, n + 1)
                need(pool, prod_ready, 4 * n)
                q = qcol[:, par, :].rearrange("p (m j r) -> p r m j", m=KC, r=8)
                for c in range(NCH):
                    last = g_.tensor_tensor(qw[:, c, :, 0:DH].rearrange("p (r m) j -> p r m j", m=KC),
                                            q[:, 4 * half:4 * half + 4, :, :],
                                            wgt[:, 0:HALF, c].rearrange("p (r m) -> p r m", m=KC).unsqueeze(3)
                                            .broadcast_to([P, 4, KC, DH]), ALU.mult)
                last.then_inc(w_qw, 1)

            def add_pieces(i, par):
                pool.wait_ge(x2_loaded, 16 * (i + 1))
                pool.wait_ge(pieces_loaded, 16 * 4 * (i + 1))
                need(pool, ffn_out, T + i - 1)
                for g in range(4):
                    src = x2_in[:, :] if g == 0 else xin[:, par, :]
                    ins = g_.tensor_tensor(xin[:, par, :], src, pieces[:, g, :], ALU.add)
                    if g < 3:
                        ins.then_inc(x3_step, 1)
                        pool.wait_ge(x3_step, 3 * i + g + 1)
                ins.then_inc(x3_ready, 1)

            def phase_b(it, par, _):
                i, i1, i2, i3 = (tile_at(it, n) for n in range(4))
                if i2 is not None:
                    normalise(T + i2, 0, ffn_mv, ffn_step, xn[:, :], xin[:, par, :], ffn_tr, T + i2).then_inc(ffn_xn, 1)
                if i1 is not None:
                    weigh_q(i1, 1 - par, 1)
                if i2 is not None:
                    square(T + i2, 0)
                    square(T + i2, 1)
                if i3 is not None:
                    neuron(T + i3, (1, 2, 3, 4))
                if i is not None:
                    weigh_q(i, par, 0)
                if i3 is not None:
                    neuron(T + i3, (5,))
                if i1 is not None:
                    add_pieces(i1, 1 - par)
            iterations(pool, phase_b)


_NAMES = ["x", "w_in", "b_in_col", "b_in_row", "w_out", "b_out", "wq", "bq_col", "wkv", "bkv_row", "temp", "w_fc", "w_proj"]


def kernel(**inputs):
    import numpy as np
    import concourse.bacc as bacc
    from concourse.bass_utils import run_bass_kernel_spmd as run

    a = {n: np.asarray(v) for n, v in inputs.items()}
    w_in = a["L0_attn_a_w_in"].reshape(H, 3, DH, D).transpose(1, 0, 2, 3).reshape(3 * D, D)
    b_in = a["L0_attn_a_b_in"].reshape(H, 3, DH).transpose(1, 0, 2).reshape(3 * D)
    laid = {
        "x": a["L0_attn_a_x"].reshape(TOK, D),
        "w_in": w_in.T,
        "b_in_col": b_in[:2 * D].reshape(2 * KC, P).T,
        "b_in_row": b_in[2 * D:].reshape(1, D),
        "w_out": a["L0_attn_a_w_out"].T,
        "b_out": a["L0_attn_a_b_out"].reshape(1, D),
        "wq": a["L0_attn_b_Wq"],
        "bq_col": a["L0_attn_b_bq"].reshape(KC, P).T,
        "wkv": np.concatenate([a["L0_attn_b_Wk"], a["L0_attn_b_Wv"]], axis=1),
        "bkv_row": np.concatenate([a["L0_attn_b_bk"], a["L0_attn_b_bv"]]).reshape(1, 2 * D),
        "temp": a["L0_attn_b_temperature"].reshape(1, H),
        "w_fc": a["L0_ffn_W_fc"].T,
        "w_proj": a["L0_ffn_W_proj"].T,
    }
    nc = bacc.Bacc("TRN2", target_bir_lowering=False, num_devices=1)
    arrays, args = {}, []
    for name in _NAMES:
        arrays["in_" + name] = np.ascontiguousarray(laid[name])
        args.append(nc.dram_tensor("in_" + name, arrays["in_" + name].shape, FP32, kind="ExternalInput").ap())
    out = nc.dram_tensor("out", (BATCH, SEQ, D), FP32, kind="ExternalOutput").ap()
    build(nc, *args, out.rearrange("b l d -> (b l) d"))
    r = run(nc, [arrays], core_ids=[0])
    return r.results[0]["out"]
```

```python
from contextlib import ExitStack

import concourse.bass as bass
from concourse import mybir

FP32 = mybir.dt.float32
BF16 = mybir.dt.bfloat16
ALU = mybir.AluOpType
ACT = mybir.ActivationFunctionType
AX = mybir.AxisListType

P = 128
BATCH, SEQ, D = 2, 2048, 256
H, DH = 16, 16
FF = 1024
KC = D // P
TOK = BATCH * SEQ
T = TOK // P
TPB = SEQ // P
GROUP = 512
NG = TOK // GROUP
SUB = GROUP // P
BANK = 512
CH = 1024
NCH = SEQ // CH
CPT = H * NCH
NBUF = 3
HALF = H // 2
EPS = 1e-5
BETA, THRESHOLD, STEPS = 0.9, 1.0, 5
PARTS = 3
Q_SLOTS = [0, 0, 0, 1, 1, 1, 2, 2]
K_SLOTS = [0, 1, 2, 0, 1, 2, 0, 1]
DRAIN = 3
LIF_OPS = 1 + 5 * (STEPS - 1)
N_PRELUDE_LOADS, N_WEIGHT_LOADS = 5, 8
UP_A, UP_B = [18, 19, 20, 21, 22, 23, 24, 25], [3, 4, 5, 5, 8, 8, 11, 11]
KV_A, Q_A = [13, 14, 15, 16], [18, 20]
DOWN_A, DOWN_B = [26, 27, 28, 28, 29, 30, 31, 31], [14, 14, 17, 17, 18, 18, 19, 20]
PROD_AT = [6, 7, 9, 10, 12, 13, 15, 16], [22, 23, 25, 26, 28, 29, 31, 32]


def build(nc, x, w_in, b_in_col, b_in_row, w_out, b_out, wq, bq_col, wkv, bkv_row, temp, w_fc, w_proj, out):
    q_parts = nc.dram_tensor("q_parts", (PARTS, D, TOK), BF16).ap()
    k_parts = nc.dram_tensor("k_parts", (PARTS, D, TOK), BF16).ap()
    v_rows = nc.dram_tensor("v_rows", (TOK, D), FP32).ap()
    x2_rows = nc.dram_tensor("x2_rows", (TOK, D), FP32).ap()
    kb_parts = nc.dram_tensor("kb_parts", (PARTS, TOK, D), BF16).ap()
    vb_parts = nc.dram_tensor("vb_parts", (PARTS, TOK, D), BF16).ap()
    qb_cols = nc.dram_tensor("qb_cols", (T * P, D), FP32).ap()

    ctx = ExitStack()
    with ctx:
        def sb(name, shape, dt=FP32):
            return ctx.enter_context(nc.sbuf_tensor(name, shape, dt))

        def pb(name, shape):
            return ctx.enter_context(nc.psum_tensor(name, shape, FP32))

        def sem(name):
            return ctx.enter_context(nc.semaphore(name))

        big = sb("big", [P, H * SEQ])
        keys = big[:, :].bitcast(BF16).rearrange("p (b h m) -> p b h m", b=BATCH, h=H)
        expo = big[:, :].rearrange("p (t s) -> p t s", t=H)
        at = 0

        def carve(n):
            nonlocal at
            at += n
            return big[:, at - n:at]
        px = carve(SUB * D).rearrange("p (s d) -> p s d", s=SUB)
        pxn = carve(SUB * D).rearrange("p (s d) -> p s d", s=SUB)
        pxT = carve(KC * GROUP).rearrange("p (k n) -> p k n", k=KC)
        pqk = carve(2 * KC * GROUP).rearrange("p (m n) -> p m n", m=2 * KC)
        pres = carve(2 * KC * GROUP).rearrange("p (m n) -> p m n", m=2 * KC)
        pparts = carve(PARTS * KC * GROUP).bitcast(BF16).rearrange("p (a m n) -> p a m n", a=PARTS, m=2 * KC)
        pv_sb = carve(SUB * D).rearrange("p (s d) -> p s d", s=SUB)
        pstat = carve(SUB * 6).rearrange("p (s k) -> p s k", s=SUB)
        pmv = carve(SUB * 2).rearrange("p (s k) -> p s k", s=SUB)
        prstd = carve(SUB)
        pvar = carve(SUB)
        bias_res = carve(4 * D)[0:1, :]
        bias_parts = [carve(2 * D)[0:1, :].bitcast(BF16) for _ in range(PARTS)]
        w_in_sb = carve(KC * 3 * D).rearrange("p (k n) -> p k n", k=KC)


        w_out_sb = sb("w_out_sb", [P, KC, D])
        wq_sb = sb("wq_sb", [P, KC, D])
        wkv_sb = sb("wkv_sb", [P, KC, 2 * D])
        w_fc_sb = sb("w_fc_sb", [P, KC, FF])
        w_proj_sb = sb("w_proj_sb", [P, FF // P, D])
        bin_col = sb("bin_col", [P, 2 * KC])
        bq_scaled = sb("bq_scaled", [P, KC])
        bqb_col = sb("bqb_col", [P, KC])
        temp_sb = sb("temp_sb", [P, T])
        ident = sb("ident", [P, P])
        ones = sb("ones", [PARTS, P], BF16)
        bias = sb("bias", [PARTS, 4 * D], BF16)
        power = sb("power", [P, SUB])

        shared = sb("shared", [P, 4 * SEQ // 2])
        qstack = shared[:, 0:2 * H * P // 2].bitcast(BF16).rearrange("p (r h n) -> p r h n", r=2, h=H)
        kvf = shared[:, 2048:2560]
        kvres = shared[:, 2560:3072]
        kvparts = shared[:, 3072:3840].bitcast(BF16).rearrange("p (a n) -> p a n", a=PARTS)
        bstack = shared[:, :].bitcast(BF16).rearrange("p (r a n) -> p r a n", r=2, a=2)
        shared2 = sb("shared2", [P, SEQ])
        xa = shared2[:, 0:512].rearrange("p (r d) -> p r d", r=2)
        va = shared2[:, 512:1024].rearrange("p (r d) -> p r d", r=2)
        opt = shared2[:, 1024:1280]
        optT = shared2[:, 1280:1536].rearrange("p (k n) -> p k n", k=KC)
        xn2 = shared2[:, 1536:1792]
        xn2T = shared2[:, 1792:2048].rearrange("p (k n) -> p k n", k=KC)
        prod = shared2[:, :]

        qcol = sb("qcol", [P, 2, D])
        pieces = sb("pieces", [P, 4, D])
        row_bias = pieces[0:1, :, :].rearrange("o a d -> o (a d)")
        x2_in = sb("x2_in", [P, D])
        qw = sb("qw", [P, NCH, HALF, 2 * DH])
        xin = sb("xin", [P, 2, D])
        xout = sb("xout", [P, 2, D])
        xn = sb("xn", [P, D])
        xnT = sb("xnT", [P, KC, P])
        hid = sb("hid", [P, FF])
        y = sb("y", [P, 2, D])
        mem = sb("mem", [P, D])
        spk = sb("spk", [P, D])
        cnt = sb("cnt", [P, D])
        nmax = sb("nmax", [P, 2, H, NCH])
        esum = sb("esum", [P, 2, H, NCH])
        nrow = sb("nrow", [P, H])
        dlt = sb("dlt", [P, H, NCH])
        fac = sb("fac", [P, H, NCH])
        sume = sb("sume", [P, H, NCH])
        tot = sb("tot", [P, H])
        rec = sb("rec", [P, H])
        wgt = sb("wgt", [P, H, NCH])
        wsum = sb("wsum", [P, H])
        st = sb("st", [P, 2, 6])
        mv = sb("mv", [P, 2, 2])
        var = sb("var", [P, 2])
        rstd = sb("rstd", [P, 2])

        score = [pb(f"score{n}", [P, CH]) for n in range(NBUF)]
        bank_f = pb("bank_f", [P, BANK])
        bank_g = pb("bank_g", [P, BANK])

        w_in_loaded, bias_split, bias_loaded = sem("w_in_loaded"), sem("bias_split"), sem("bias_loaded")
        att_step, ffn_step, qkv_step, w_step = (sem(n) for n in ("att_step", "ffn_step", "qkv_step", "w_step"))
        w_loaded, consts, ident0, bq_ready = sem("w_loaded"), sem("consts"), sem("ident0"), sem("bq_ready")
        px_loaded, p_stats, p_aggr, p_rstd, p_xn = (sem(n) for n in ("px_loaded", "p_stats", "p_aggr", "p_rstd", "p_xn"))
        p_tr, p_xT, p_qk, p_qkf, p_v, p_vs = (sem(n) for n in ("p_tr", "p_xT", "p_qk", "p_qkf", "p_v", "p_vs"))
        p_split, p_stored = sem("p_split"), sem("p_stored")
        keys_loaded = [sem(f"keys_loaded{b}") for b in range(BATCH)]
        q_loaded = [sem(f"q_loaded{r}") for r in range(2)]
        xv_loaded = [sem(f"xv_loaded{r}") for r in range(2)]
        scores_a, max_a, exp_a = sem("scores_a"), sem("max_a"), sem("exp_a")
        att_min, att_dlt, att_fac, att_sum, att_rec, att_opt = (
            sem(n) for n in ("att_min", "att_dlt", "att_fac", "att_sum", "att_rec", "att_opt"))
        opt_tr, opt_T, oproj = sem("opt_tr"), sem("opt_T"), sem("oproj")
        ffn_x1 = sem("ffn_x1")
        ffn_stats, ffn_mv, ffn_xn, ffn_tr, ffn_xT = (sem(n) for n in ("ffn_stats", "ffn_mv", "ffn_xn", "ffn_tr", "ffn_xT"))
        ffn_fc, ffn_relu, ffn_sq, ffn_y, ffn_ysb = (sem(n) for n in ("ffn_fc", "ffn_relu", "ffn_sq", "ffn_y", "ffn_ysb"))
        lif, ffn_out = sem("lif"), sem("ffn_out")
        qkv_stats, qkv_mv, qkv_xn, qkv_tr, qkv_xT = (sem(n) for n in ("qkv_stats", "qkv_mv", "qkv_xn", "qkv_tr", "qkv_xT"))
        qkv_kv, qkv_kvf, qkv_q, qkv_qf, qkv_split = (sem(n) for n in ("qkv_kv", "qkv_kvf", "qkv_q", "qkv_qf", "qkv_split"))
        parts_stored = sem("parts_stored")
        x2_stored, qb_stored = ([sem(f"{n}{r}") for r in range(2)] for n in ("x2_stored", "qb_stored"))
        b_loaded = [sem(f"b_loaded{r}") for r in range(2)]
        x2_loaded = sem("x2_loaded")
        scores_b, max_b, exp_b = sem("scores_b"), sem("max_b"), sem("exp_b")
        w_min, w_dlt, w_fac, w_sum, w_rec, w_qw = (sem(n) for n in ("w_min", "w_dlt", "w_fac", "w_sum", "w_rec", "w_qw"))
        prod_ready, prod_kept, prod_added = sem("prod_ready"), sem("prod_kept"), sem("prod_added")
        pieces_loaded, x3_step, x3_ready = sem("pieces_loaded"), sem("x3_step"), sem("x3_ready")
        out_stored = [sem(f"out_stored{r}") for r in range(2)]

        block = ctx.enter_context(nc.Block())

        def need(eng, s, value):
            if not (isinstance(value, int) and value <= 0):
                eng.wait_ge(s, value)

        def stand_alone(eng, *waits):
            waits = [(s, n if isinstance(n, int) else eng.to_reg(n)) for s, n in waits]
            eng.wait_ge(consts, 4)
            for s, n in waits:
                need(eng, s, n)

        def tile_at(it, lag):
            if isinstance(it, int) and not 0 <= it - lag < T:
                return None
            return it - lag

        def iterations(eng, body, cuts=(T,)):
            for it in range(6):
                body(it, it % 2, 0)
            low = 6
            for n, cut in enumerate(cuts):
                with eng.Fori(low, cut, 2) as it:
                    body(it, 0, n)
                    body(it + 1, 1, n)
                low = cut
            for it in range(low, T + DRAIN):
                body(it, it % 2, len(cuts) - 1)

        order = [0, 1, 2] * (CPT // NBUF) + [0, 1, 0]
        order += ([2, 1, 0] * CPT)[:2 * CPT - len(order)]
        last_use = [next(d for d in range(1, 2 * CPT) if order[q - d] == order[q]) for q in range(2 * CPT)]

        def chunk_buffer(par, c):
            return order[CPT * par + c], last_use[CPT * par + c]

        @block.sync
        def _(sp):
            loads = [
                (row_bias[:, 0:D], b_in_row),
                (row_bias[:, D:2 * D], b_out),
                (row_bias[:, 2 * D:4 * D], bkv_row),
                (w_in_sb, w_in.rearrange("(k p) n -> p k n", p=P)),
                (bin_col[:, :], b_in_col),
                (w_out_sb[:, :, :], w_out.rearrange("(k p) n -> p k n", p=P)),
                (wq_sb[:, :, :], wq.rearrange("(k p) n -> p k n", p=P)),
                (bqb_col[:, :], bq_col),
                (wkv_sb[:, :, :], wkv.rearrange("(k p) n -> p k n", p=P)),
                (temp_sb[:, 0:H], temp.broadcast_to([P, H])),
                (temp_sb[:, H:2 * H], temp.broadcast_to([P, H])),
                (w_fc_sb[:, :, :], w_fc.rearrange("(k p) n -> p k n", p=P)),
                (w_proj_sb[:, :, :], w_proj.rearrange("(k p) n -> p k n", p=P)),
            ]
            assert len(loads) == N_PRELUDE_LOADS + N_WEIGHT_LOADS

            def load_x(g):
                sp.dma_start(px, x[bass.ds(g * GROUP, GROUP), :].rearrange("(s p) d -> p s d", p=P)).then_inc(px_loaded, 16)

            def store_group(g):
                cols = bass.ds(g * GROUP, GROUP)
                stand_alone(sp, (p_vs, g + 1))
                sp.dma_start(v_rows[cols, :].rearrange("(s p) d -> p s d", p=P), pv_sb).then_inc(p_stored, 16)
                stand_alone(sp, (p_split, 4 * g + 4))
                for a in range(PARTS):
                    sp.dma_start(q_parts[a, :, cols].rearrange("(m p) n -> p m n", p=P), pparts[:, a, 0:KC, :]).then_inc(p_stored, 16)
                    sp.dma_start(k_parts[a, :, cols].rearrange("(m p) n -> p m n", p=P), pparts[:, a, KC:2 * KC, :]).then_inc(p_stored, 16)

            load_x(0)
            for n, (dst, src) in enumerate(loads):
                sp.dma_start(dst, src).then_inc(w_in_loaded if n < N_PRELUDE_LOADS else w_loaded, 16)
            sp.wait_ge(bias_split, 4)
            for a in range(PARTS):
                sp.dma_start(bias[a:a + 1, :], bias_parts[a]).then_inc(bias_loaded, 16)
            with sp.Fori(0, NG - 1) as g:
                stand_alone(sp, (p_xn, g + 1))
                load_x(g + 1)
                store_group(g)
            store_group(NG - 1)

            sp.wait_ge(p_stored, 16 * 7 * NG)
            sp.wait_ge(p_qk, 4 * NG)
            sp.wait_ge(p_v, NG)

            def load_q(i, par):
                for s in range(8):
                    src = q_parts[Q_SLOTS[s], :, bass.ds(i * P, P)].rearrange("(h d) n -> d h n", d=DH)
                    sp.dma_start(qstack[s * DH:(s + 1) * DH, par, :, :], src).then_inc(q_loaded[par], 16)

            for b in range(BATCH):
                for s in range(8):
                    src = k_parts[K_SLOTS[s], :, b * SEQ:(b + 1) * SEQ].rearrange("(h d) m -> d h m", d=DH)
                    sp.dma_start(keys[s * DH:(s + 1) * DH, b, :, :], src).then_inc(keys_loaded[b], 16)
                if b == 0:
                    load_q(0, 0)

            def phase_a(it, par, _):
                i = tile_at(it, 0)
                if i is not None:
                    if not (isinstance(i, int) and i == T - 1):
                        stand_alone(sp, (scores_a, CPT * i))
                        load_q(i + 1, 1 - par)
                    stand_alone(sp, (att_opt, i - 1), (ffn_x1, i - 1))
                    sp.dma_start(xa[:, par, :], x[bass.ds(i * P, P), :]).then_inc(xv_loaded[par], 16)
                    sp.dma_start(va[:, par, :], v_rows[bass.ds(i * P, P), :]).then_inc(xv_loaded[par], 16)
                i = tile_at(it, 3)
                if i is not None:
                    r = (par + 1) % 2
                    row = bass.ds(i * P, P)
                    stand_alone(sp, (ffn_out, i + 1))
                    sp.dma_start(x2_rows[row, :], xout[:, r, :]).then_inc(x2_stored[r], 16)
                    stand_alone(sp, (qkv_qf, i + 1))
                    sp.dma_start(qb_cols[row, :], qcol[:, r, :]).then_inc(qb_stored[r], 16)
                    stand_alone(sp, (qkv_split, 4 * i + 4))
                    for a in range(PARTS):
                        sp.dma_start(kb_parts[a, row, :], kvparts[:, a, 0:D]).then_inc(parts_stored, 16)
                        sp.dma_start(vb_parts[a, row, :], kvparts[:, a, D:2 * D]).then_inc(parts_stored, 16)
            iterations(sp, phase_a, (T - 2,))

            for r in range(2):
                sp.wait_ge(x2_stored[r], 16 * T // 2)
                sp.wait_ge(qb_stored[r], 16 * T // 2)
            sp.wait_ge(parts_stored, 16 * 2 * PARTS * T)

            def load_b(i, par):
                for s in range(8):
                    for side, (parts, slots) in enumerate(((kb_parts, Q_SLOTS), (vb_parts, K_SLOTS))):
                        src = parts[slots[s], bass.ds(i * P, P), :].rearrange("(r j) d -> r (j d)", r=DH)
                        sp.dma_start(bstack[s * DH:(s + 1) * DH, par, side, :], src).then_inc(b_loaded[par], 16)
                sp.dma_start(qcol[:, par, :], qb_cols[bass.ds(i * P, P), :]).then_inc(b_loaded[par], 16)
            sp.wait_ge(scores_a, CPT * T)
            load_b(0, 0)

            def phase_b(it, par, _):
                i = tile_at(it, 0)
                if i is not None and not (isinstance(i, int) and i == T - 1):
                    stand_alone(sp, (scores_b, CPT * i), (w_qw, 2 * i))
                    load_b(i + 1, 1 - par)
                i = tile_at(it, 1)
                if i is not None:
                    stand_alone(sp, (x3_ready, i))
                    sp.dma_start(x2_in[:, :], x2_rows[bass.ds(i * P, P), :]).then_inc(x2_loaded, 16)
                    stand_alone(sp, (prod_added, 4 * i + 4))
                    for g in range(4):
                        sp.dma_start(pieces[:, g, :], prod[32 * g:32 * g + DH, :].rearrange("r (j d) -> r j d", j=8)) \
                          .then_inc(pieces_loaded, 16)
                i = tile_at(it, 3)
                if i is not None:
                    r = (par + 1) % 2
                    stand_alone(sp, (ffn_out, T + i + 1))
                    sp.dma_start(out[bass.ds(i * P, P), :], xout[:, r, :]).then_inc(out_stored[r], 16)
            iterations(sp, phase_b, (T - 2,))
            for r in range(2):
                sp.wait_ge(out_stored[r], 16 * T // 2)

        @block.tensor
        def _(pe):
            mm = nc.tensor.matmul

            def transpose2(dst, src):
                for k in range(KC):
                    last = nc.tensor.transpose(dst[:, k * P:(k + 1) * P], src[:, k * P:(k + 1) * P], ident[:, :])
                return last

            pe.wait_ge(w_in_loaded, 16 * N_PRELUDE_LOADS)
            pe.wait_ge(consts, 4)
            pe.wait_ge(bias_loaded, 16 * PARTS)

            def tr(g):
                pe.wait_ge(p_xn, g + 1)
                need(pe, p_xT, g)
                for k in range(KC):
                    for s in range(SUB):
                        last = nc.tensor.transpose(score[0][:, k * GROUP + s * P:k * GROUP + (s + 1) * P],
                                                   pxn[:, s, k * P:(k + 1) * P], ident[:, :])
                last.then_inc(p_tr, 1)

            def project(g):
                pe.wait_ge(p_xT, g + 1)
                need(pe, p_qkf, g)
                for m in range(2 * KC):
                    dst = score[1 + m // 2][:, (m % 2) * GROUP:(m % 2 + 1) * GROUP]
                    for k in range(KC):
                        last = mm(dst, w_in_sb[:, k, m * P:(m + 1) * P], pxT[:, k, :], start=(k == 0), stop=(k == KC - 1))
                    last.then_inc(p_qk, 1)
                need(pe, p_vs, g)
                for s in range(SUB):
                    dst = (bank_f, bank_g)[s // 2][:, (s % 2) * D:(s % 2 + 1) * D]
                    for k in range(KC):
                        mm(dst, pxT[:, k, s * P:(s + 1) * P], w_in_sb[:, k, 2 * D:3 * D], start=(k == 0), stop=False)
                    last = mm(dst, ones[:, :], bias[:, 0:D], start=False, stop=True)
                last.then_inc(p_v, 1)
            tr(0)
            tr(1)
            project(0)
            with pe.Fori(1, NG - 1) as g:
                tr(g + 1)
                project(g)
            project(NG - 1)
            pe.wait_ge(p_qkf, NG)
            pe.wait_ge(p_vs, NG)
            pe.wait_ge(w_loaded, 16 * N_WEIGHT_LOADS)

            def ffn_transpose(n):
                pe.wait_ge(ffn_xn, n + 1)
                need(pe, ffn_ysb, n)
                transpose2(bank_f, xn).then_inc(ffn_tr, 1)

            def ffn_up(n, f):
                if f == 0:
                    pe.wait_ge(ffn_xT, n + 1)
                if f == 4:
                    pe.wait_ge(ffn_relu, 2 * n + 1)
                for k in range(KC):
                    last = mm(bank_f[:, (f % 4) * P:(f % 4 + 1) * P], w_fc_sb[:, k, f * P:(f + 1) * P], xnT[:, k, :],
                              start=(k == 0), stop=(k == KC - 1))
                if f % 4 == 3:
                    last.then_inc(ffn_fc, 1)

            def ffn_down(n, f):
                if f == 0:
                    pe.wait_ge(ffn_relu, 2 * n + 2)
                if f % 4 == 0:
                    pe.wait_ge(ffn_sq, 2 * n + f // 4 + 1)
                last = mm(bank_f[:, 0:D], hid[:, f * P:(f + 1) * P], w_proj_sb[:, f, :], start=(f == 0), stop=(f == FF // P - 1))
                if f == FF // P - 1:
                    last.then_inc(ffn_y, 1)

            def phase_a(it, par, b):
                i, i1, i3 = tile_at(it, 0), tile_at(it, 1), tile_at(it, 3)
                if isinstance(it, int):
                    b = min(it, T - 1) // TPB
                if i is not None:
                    if isinstance(i, int):
                        pe.wait_ge(q_loaded[par], 128 * (i // 2 + 1))
                    else:
                        pe.wait_ge(q_loaded[par], 64 * (i - par) + 128)
                    pe.wait_ge(keys_loaded[b], 128)
                for c in range(CPT):
                    if i is not None:
                        buf, ago = chunk_buffer(par, c)
                        need(pe, exp_a, CPT * i + c - ago + 1)
                        for k in range(CH // BANK):
                            col = (c % NCH) * CH + k * BANK
                            last = mm(score[buf][:, k * BANK:(k + 1) * BANK], qstack[:, par, c // NCH, :],
                                      keys[:, b, c // NCH, col:col + BANK], start=True, stop=True)
                        last.then_inc(scores_a, 1)
                    if i3 is not None:
                        if c == 12:
                            pe.wait_ge(qkv_xn, i3 + 1)
                            need(pe, qkv_qf, i3)
                            transpose2(bank_g, xn2).then_inc(qkv_tr, 1)
                        if c in KV_A:
                            side, k = divmod(KV_A.index(c), KC)
                            cols = slice(side * D, (side + 1) * D)
                            if c == KV_A[0]:
                                pe.wait_ge(qkv_xT, i3 + 1)
                            last = mm(bank_g[:, cols], xn2T[:, k, :], wkv_sb[:, k, cols], start=(k == 0), stop=False)
                            if k == KC - 1:
                                last = mm(bank_g[:, cols], ones[:, :], bias[:, 2 * D + side * D:3 * D + side * D],
                                          start=False, stop=True)
                                if side == 1:
                                    last.then_inc(qkv_kv, 1)
                        if c in Q_A:
                            m = Q_A.index(c)
                            if m == 0:
                                pe.wait_ge(qkv_kvf, i3 + 1)
                            for k in range(KC):
                                last = mm(bank_g[:, m * P:(m + 1) * P], wq_sb[:, k, m * P:(m + 1) * P], xn2T[:, k, :],
                                          start=(k == 0), stop=(k == KC - 1))
                            if m == KC - 1:
                                last.then_inc(qkv_q, 1)
                    if i1 is not None:
                        if c == 9:
                            pe.wait_ge(att_opt, i1 + 1)
                            need(pe, ffn_ysb, i1)
                            transpose2(bank_f, opt).then_inc(opt_tr, 1)
                        if c in (10, 11):
                            k = c - 10
                            if k == 0:
                                pe.wait_ge(opt_T, i1 + 1)
                            last = mm(bank_f[:, D:2 * D], optT[:, k, :], w_out_sb[:, k, :], start=(k == 0), stop=False)
                            if k == KC - 1:
                                mm(bank_f[:, D:2 * D], ones[:, :], bias[:, D:2 * D], start=False, stop=True).then_inc(oproj, 1)
                        if c == 17:
                            ffn_transpose(i1)
                        if c in UP_A:
                            ffn_up(i1, UP_A.index(c))
                        for f in range(FF // P):
                            if c == DOWN_A[f]:
                                ffn_down(i1, f)
            iterations(pe, phase_a, (TPB, T))

            def product(i, half, sc, rr):
                if rr == 0:
                    if sc == 0:
                        pe.wait_ge(w_qw, 2 * i + half + 1)
                    if half == 0:
                        need(pe, prod_kept, 4 * i + sc)
                        if sc == 0:
                            need(pe, prod_added, 4 * i)
                            if isinstance(i, int) and i == 0:
                                pe.wait_ge(qkv_qf, T)
                    else:
                        pe.wait_ge(prod_kept, 4 * i + 4)
                        need(pe, prod_added, 4 * i + sc)
                for g in range(4):
                    n = 4 * rr + g
                    last = mm(bank_g[32 * g:32 * g + 32, :], qw[:, sc * BANK // CH, n, :],
                              expo[:, HALF * half + n, sc * BANK:(sc + 1) * BANK], start=(rr == 0), stop=(rr == 1))
                if rr == 1:
                    last.then_inc(prod_ready, 1)

            def phase_b(it, par, _):
                i, i1, i2 = tile_at(it, 0), tile_at(it, 1), tile_at(it, 2)
                if i is not None:
                    if isinstance(i, int):
                        pe.wait_ge(b_loaded[par], 16 * 17 * (i // 2 + 1))
                    else:
                        pe.wait_ge(b_loaded[par], 8 * 17 * (i - par) + 16 * 17)
                for c in range(CPT):
                    if i is not None:
                        buf, ago = chunk_buffer(par, c)
                        if isinstance(i, int) and i == 0 and c < NBUF:
                            pe.wait_ge(exp_a, CPT * T)
                        need(pe, exp_b, CPT * i + c - ago + 1)
                        row = c // NCH * P
                        for k in range(CH // BANK):
                            col = (c % NCH) * CH + k * BANK
                            last = mm(score[buf][:, k * BANK:(k + 1) * BANK], bstack[:, par, 0, row:row + P],
                                      bstack[:, par, 1, col:col + BANK], start=True, stop=True)
                        last.then_inc(scores_b, 1)
                    if i2 is not None:
                        if c == 1:
                            ffn_transpose(T + i2)
                        for f in range(FF // P):
                            if c == UP_B[f]:
                                ffn_up(T + i2, f)
                        for f in range(FF // P):
                            if c == DOWN_B[f]:
                                ffn_down(T + i2, f)
                    if i1 is not None and c == 0:
                        product(i1, 0, 3, 1)
                    if i1 is not None and c in PROD_AT[0]:
                        n = PROD_AT[0].index(c)
                        product(i1, 1, n // 2, n % 2)
                    if i is not None and c in PROD_AT[1]:
                        n = PROD_AT[1].index(c)
                        product(i, 0, n // 2, n % 2)
            iterations(pe, phase_b)

        @block.vector
        def _(dve):
            v = nc.vector
            v.memset(ones[:, :], 1.0).then_inc(consts, 1)
            v.memset(power[:, :], -0.5).then_inc(consts, 1)
            v.memset(qw[:, :, :, :], 0.0).then_inc(consts, 1)
            dve.wait_ge(w_in_loaded, 16 * N_PRELUDE_LOADS)
            v.tensor_scalar(bq_scaled[:, :], bin_col[:, 0:KC], DH ** -0.5, None, ALU.mult).then_inc(bq_ready, 1)
            v.tensor_copy(bias_parts[0], row_bias).then_inc(bias_split, 1)
            dve.wait_ge(bias_split, 1)
            v.tensor_tensor(bias_res, row_bias, bias_parts[0], ALU.subtract).then_inc(bias_split, 1)
            dve.wait_ge(bias_split, 2)
            v.tensor_copy(bias_parts[1], bias_res).then_inc(bias_split, 1)
            dve.wait_ge(bias_split, 3)
            v.tensor_tensor(bias_parts[2], bias_res, bias_parts[1], ALU.subtract).then_inc(bias_split, 1)

            def norm(g):
                dve.wait_ge(px_loaded, 16 * (g + 1))
                for s in range(SUB):
                    v.bn_stats(pstat[:, s, :], px[:, s, :]).then_inc(p_stats, 1)
                need(dve, p_rstd, 2 * g)
                for s in range(SUB):
                    stand_alone(dve, (p_stats, SUB * g + s + 1))
                    v.bn_aggr(pmv[:, s, :], pstat[:, s, :]).then_inc(p_aggr, 1)
                dve.wait_ge(p_rstd, 2 * g + 2)
                need(dve, p_tr, g)
                dve.wait_ge(p_aggr, SUB * g + SUB)
                for s in range(SUB):
                    last = v.tensor_scalar(pxn[:, s, :], px[:, s, :], pmv[:, s, 0:1], prstd[:, s:s + 1], ALU.subtract, ALU.mult)
                last.then_inc(p_xn, 1)

            def split(g):
                dve.wait_ge(p_qkf, g + 1)
                need(dve, p_stored, 16 * 7 * g)
                v.tensor_copy(pparts[:, 0, :, :], pqk).then_inc(p_split, 1)
                dve.wait_ge(p_split, 4 * g + 1)
                v.tensor_tensor(pres, pqk, pparts[:, 0, :, :], ALU.subtract).then_inc(p_split, 1)
                dve.wait_ge(p_split, 4 * g + 2)
                v.tensor_copy(pparts[:, 1, :, :], pres).then_inc(p_split, 1)
                dve.wait_ge(p_split, 4 * g + 3)
                v.tensor_tensor(pparts[:, 2, :, :], pres, pparts[:, 1, :, :], ALU.subtract).then_inc(p_split, 1)
            norm(0)
            norm(1)
            split(0)
            with dve.Fori(1, NG - 1) as g:
                norm(g + 1)
                split(g)
            split(NG - 1)

            def ffn_norm(n, par, done, count):
                dve.wait_ge(done, count)
                v.bn_stats(st[:, 0, :], xin[:, par, :]).then_inc(ffn_stats, 1)
                stand_alone(dve, (ffn_stats, n + 1), (ffn_xn, n))
                v.bn_aggr(mv[:, 0, :], st[:, 0, :]).then_inc(ffn_mv, 1)

            def ffn_result(n, par, stored, count):
                dve.wait_ge(lif, LIF_OPS * (n + 1))
                need(dve, stored, count)
                v.scalar_tensor_tensor(out=xout[:, par, :], in0=cnt[:, :], scalar=1.0 / STEPS, in1=xin[:, par, :],
                                       op0=ALU.mult, op1=ALU.add).then_inc(ffn_out, 1)

            def phase_a(it, par, _):
                i, i1, i3 = tile_at(it, 0), tile_at(it, 1), tile_at(it, 3)
                r1, r3 = 1 - par, 1 - par
                for c in range(CPT):
                    if i is not None:
                        if c == 0:
                            need(dve, att_dlt, i - 1)
                        dve.wait_ge(scores_a, CPT * i + c + 1)
                        v.tensor_reduce(nmax[:, par, c // NCH, c % NCH:c % NCH + 1], score[chunk_buffer(par, c)[0]][:, :],
                                        AX.X, ALU.max, negate=True).then_inc(max_a, 1)
                    if i1 is not None:
                        if c == 0:
                            dve.wait_ge(max_a, CPT * i1 + CPT)
                            need(dve, att_dlt, i1)
                            v.tensor_tensor(nrow[:, :], nmax[:, r1, :, 0], nmax[:, r1, :, 1], ALU.min).then_inc(att_min, 1)
                        if c == 4:
                            dve.wait_ge(att_sum, 2 * i1 + 2)
                            v.reciprocal(rec[:, :], tot[:, :]).then_inc(att_rec, 1)
                        if c == 11:
                            dve.wait_ge(oproj, i1 + 1)
                            need(dve, ffn_out, i1 - 1)
                            if isinstance(i1, int):
                                dve.wait_ge(xv_loaded[r1], 32 * (i1 // 2 + 1))
                            else:
                                dve.wait_ge(xv_loaded[r1], 16 * (i1 - r1) + 32)
                            v.tensor_tensor(xin[:, r1, :], bank_f[:, D:2 * D], xa[:, r1, :], ALU.add).then_inc(ffn_x1, 1)
                        if c == 12:
                            ffn_norm(i1, r1, ffn_x1, i1 + 1)
                    if i3 is not None and c == 5:
                        need(dve, qkv_xn, i3 - 1)
                        ffn_result(i3, r3, x2_stored[r3], 8 * (i3 - r3))
                    if i3 is not None and c == 6:
                        dve.wait_ge(ffn_out, i3 + 1)
                        v.bn_stats(st[:, 1, :], xout[:, r3, :]).then_inc(qkv_stats, 1)
                        stand_alone(dve, (qkv_stats, i3 + 1), (qkv_xn, i3))
                        v.bn_aggr(mv[:, 1, :], st[:, 1, :]).then_inc(qkv_mv, 1)
            iterations(dve, phase_a)

            def row_min(i, par, half):
                t0 = HALF * half
                dve.wait_ge(max_b, CPT * i + CPT // 2 * (half + 1))
                need(dve, w_dlt, 2 * i + half)
                v.tensor_tensor(nrow[:, 0:HALF], nmax[:, par, t0:t0 + HALF, 0], nmax[:, par, t0:t0 + HALF, 1], ALU.min) \
                    .then_inc(w_min, 1)

            def row_rec(i, half):
                dve.wait_ge(w_sum, 2 * (2 * i + half) + 2)
                v.reciprocal(rec[:, 0:HALF], tot[:, 0:HALF]).then_inc(w_rec, 1)

            def phase_b(it, par, _):
                i, i1, i2, i3 = (tile_at(it, n) for n in range(4))
                for c in range(CPT):
                    if i is not None:
                        if c == 0:
                            need(dve, w_dlt, 2 * (i - 1))
                            if isinstance(i, int) and i == 0:
                                dve.wait_ge(att_dlt, T)
                        dve.wait_ge(scores_b, CPT * i + c + 1)
                        v.tensor_reduce(nmax[:, par, c // NCH, c % NCH:c % NCH + 1], score[chunk_buffer(par, c)[0]][:, :],
                                        AX.X, ALU.max, negate=True).then_inc(max_b, 1)
                    if i1 is not None:
                        if c == 2:
                            row_rec(i1, 1)
                        for sc in range(4):
                            if c == PROD_AT[0][2 * sc + 1]:
                                dve.wait_ge(prod_ready, 8 * i1 + 4 + sc + 1)
                                dve.wait_ge(prod_kept, 4 * i1 + sc + 1)
                                cols = prod[:, sc * BANK:(sc + 1) * BANK]
                                v.tensor_tensor(cols, bank_g[:, :], cols, ALU.add).then_inc(prod_added, 1)
                        if c == 27:
                            ffn_norm(T + i1, 1 - par, x3_ready, i1 + 1)
                    if i is not None:
                        if c == 15:
                            row_min(i, par, 0)
                        if c == 18:
                            row_rec(i, 0)
                        if c == 31:
                            row_min(i, par, 1)
                    if i3 is not None and c == 20:
                        if isinstance(i3, int) and i3 < 2:
                            dve.wait_ge(x2_stored[1 - par], 16 * T // 2)
                            dve.wait_ge(qkv_xn, T)
                        ffn_result(T + i3, 1 - par, out_stored[1 - par], 8 * (i3 - (1 - par)))
            iterations(dve, phase_b)

        @block.scalar
        def _(act):
            a = nc.scalar
            act.wait_ge(bq_ready, 1)
            act.wait_ge(w_in_loaded, 16 * N_PRELUDE_LOADS)

            def group(g):
                act.wait_ge(p_tr, g + 1)
                need(act, p_v, g)
                for k in range(KC):
                    last = a.activation(pxT[:, k, :], score[0][:, k * GROUP:(k + 1) * GROUP], ACT.Copy)
                last.then_inc(p_xT, 1)
                need(act, p_split, 4 * g)
                for m in range(2 * KC):
                    act.wait_ge(p_qk, 4 * g + m + 1)
                    src = score[1 + m // 2][:, (m % 2) * GROUP:(m % 2 + 1) * GROUP]
                    if m < KC:
                        last = a.activation(pqk[:, m, :], src, ACT.Identity, bias=bq_scaled[:, m:m + 1], scale=DH ** -0.5)
                    else:
                        last = a.activation(pqk[:, m, :], src, ACT.Identity, bias=bin_col[:, m:m + 1])
                last.then_inc(p_qkf, 1)
                act.wait_ge(p_v, g + 1)
                need(act, p_stored, 16 * 7 * g)
                a.activation(pv_sb[:, 0:2, :], bank_f[:, :].rearrange("p (s d) -> p s d", s=2), ACT.Copy)
                a.activation(pv_sb[:, 2:4, :], bank_g[:, :].rearrange("p (s d) -> p s d", s=2), ACT.Copy).then_inc(p_vs, 1)
            group(0)
            with act.Fori(1, NG) as g:
                group(g)

            def ffn_columns(n):
                act.wait_ge(ffn_tr, n + 1)
                need(act, ffn_fc, 2 * n)
                a.activation(xnT[:, :, :], bank_f[:, 0:D].rearrange("p (k n) -> p k n", k=KC), ACT.Copy).then_inc(ffn_xT, 1)

            def ffn_act(n, part):
                act.wait_ge(ffn_fc, 2 * n + part + 1)
                if part == 0:
                    need(act, ffn_y, n)
                a.activation(hid[:, part * BANK:(part + 1) * BANK], bank_f[:, :], ACT.Relu).then_inc(ffn_relu, 1)

            def ffn_take(n, r):
                act.wait_ge(ffn_y, n + 1)
                need(act, lif, LIF_OPS * (n - 1))
                a.activation(y[:, r, :], bank_f[:, 0:D], ACT.Copy).then_inc(ffn_ysb, 1)

            act.wait_ge(w_loaded, 16 * N_WEIGHT_LOADS)

            def phase_a(it, par, _):
                i, i1, i3 = tile_at(it, 0), tile_at(it, 1), tile_at(it, 3)
                for c in range(CPT):
                    if i is not None:
                        if c == 0:
                            need(act, att_sum, 2 * (i - 1))
                        act.wait_ge(max_a, CPT * i + c + 1)
                        s = score[chunk_buffer(par, c)[0]]
                        a.activation(s[:, :], s[:, :], ACT.Exp, bias=nmax[:, par, c // NCH, c % NCH:c % NCH + 1],
                                     accum_out=esum[:, par, c // NCH, c % NCH:c % NCH + 1]).then_inc(exp_a, 1)
                    if i1 is not None:
                        if c == 1:
                            act.wait_ge(att_dlt, i1 + 1)
                            need(act, att_sum, 2 * i1)
                            a.activation(fac[:, :, :], dlt[:, :, :], ACT.Exp).then_inc(att_fac, 1)
                        if c == 7:
                            act.wait_ge(opt_tr, i1 + 1)
                            a.activation(optT[:, :, :], bank_f[:, 0:D].rearrange("p (k n) -> p k n", k=KC), ACT.Copy) \
                                .then_inc(opt_T, 1)
                        if c == 15:
                            ffn_columns(i1)
                        if c == 19:
                            ffn_act(i1, 0)
                        if c == 23:
                            ffn_act(i1, 1)
                        if c == 29:
                            ffn_take(i1, 1 - par)
                    if i3 is not None:
                        r = 1 - par
                        if c == 10:
                            act.wait_ge(qkv_tr, i3 + 1)
                            need(act, qkv_q, i3)
                            a.activation(xn2T[:, :, :], bank_g[:, 0:D].rearrange("p (k n) -> p k n", k=KC), ACT.Copy) \
                                .then_inc(qkv_xT, 1)
                        if c == 15:
                            act.wait_ge(qkv_kv, i3 + 1)
                            need(act, qkv_split, 4 * i3)
                            a.activation(kvf[:, 0:D], bank_g[:, 0:D], ACT.Copy, scale=temp_sb[:, bass.ds(i3, 1)])
                            a.activation(kvf[:, D:2 * D], bank_g[:, D:2 * D], ACT.Copy).then_inc(qkv_kvf, 1)
                        if c == 20:
                            act.wait_ge(qkv_q, i3 + 1)
                            need(act, qb_stored[r], 8 * (i3 - r))
                            for m in range(KC):
                                last = a.activation(qcol[:, r, m * P:(m + 1) * P], bank_g[:, m * P:(m + 1) * P], ACT.Identity,
                                                    bias=bqb_col[:, m:m + 1])
                            last.then_inc(qkv_qf, 1)
            iterations(act, phase_a)

            def row_fac(i, half):
                act.wait_ge(w_dlt, 2 * i + half + 1)
                need(act, w_qw, 2 * i + half)
                a.activation(fac[:, 0:HALF, :], dlt[:, 0:HALF, :], ACT.Exp).then_inc(w_fac, 1)

            def phase_b(it, par, _):
                i, i2 = tile_at(it, 0), tile_at(it, 2)
                for c in range(CPT):
                    if i is not None:
                        if c == 0:
                            need(act, w_sum, 2 * 2 * (i - 1))
                            if isinstance(i, int) and i == 0:
                                act.wait_ge(att_sum, 2 * T)
                            need(act, prod_ready, 8 * (i - 1) + 4)
                        if c == CPT // 2:
                            need(act, prod_ready, 8 * i)
                        act.wait_ge(max_b, CPT * i + c + 1)
                        a.activation(expo[:, c // NCH, (c % NCH) * CH:(c % NCH + 1) * CH], score[chunk_buffer(par, c)[0]][:, :],
                                     ACT.Exp, bias=nmax[:, par, c // NCH, c % NCH:c % NCH + 1],
                                     accum_out=esum[:, par, c // NCH, c % NCH:c % NCH + 1]).then_inc(exp_b, 1)
                    if i2 is not None:
                        if c == 0:
                            ffn_columns(T + i2)
                        if c == 4:
                            ffn_act(T + i2, 0)
                        if c == 10:
                            ffn_act(T + i2, 1)
                        if c == 19:
                            ffn_take(T + i2, par)
                    if i is not None:
                        if c == 15:
                            row_fac(i, 0)
                        if c == 31:
                            row_fac(i, 1)
                        for sc in range(4):
                            if c == PROD_AT[1][2 * sc + 1] - 1:
                                act.wait_ge(prod_ready, 8 * i + sc + 1)
                                need(act, pieces_loaded, 16 * 4 * i)
                                a.activation(prod[:, sc * BANK:(sc + 1) * BANK], bank_g[:, :], ACT.Copy).then_inc(prod_kept, 1)
            iterations(act, phase_b)

        @block.gpsimd
        def _(pool):
            g_ = nc.gpsimd
            g_.memset(ident[:, :], 0.0).then_inc(ident0, 1)
            pool.wait_ge(ident0, 1)
            g_.affine_select(out=ident[:, :], in_=ident[:, :], compare_op=ALU.not_equal, fill=1.0, base=0,
                             pattern=[[-1, P]], channel_multiplier=1).then_inc(consts, 1)
            pool.wait_ge(consts, 4)

            def group_rstd(g):
                stand_alone(pool, (p_aggr, SUB * g + SUB), (p_xn, g))
                g_.tensor_scalar(pvar, pmv[:, :, 1], EPS, 0.0, ALU.add, ALU.add).then_inc(p_rstd, 1)
                pool.wait_ge(p_rstd, 2 * g + 1)
                g_.tensor_tensor(prstd, pvar, power[:, 0:SUB], ALU.pow).then_inc(p_rstd, 1)
            group_rstd(0)
            with pool.Fori(1, NG) as g:
                group_rstd(g)

            def normalise(n, which, got, step, dst, src, free, count):
                stand_alone(pool, (got, n + 1))
                g_.tensor_scalar(var[:, which:which + 1], mv[:, which, 1:2], EPS, 0.0, ALU.add, ALU.add).then_inc(step, 1)
                pool.wait_ge(step, 2 * n + 1)
                g_.tensor_tensor(rstd[:, which:which + 1], var[:, which:which + 1], power[:, 0:1], ALU.pow).then_inc(step, 1)
                stand_alone(pool, (step, 2 * n + 2), (free, count))
                return g_.tensor_scalar(dst, src, mv[:, which, 0:1], rstd[:, which:which + 1], ALU.subtract, ALU.mult)

            def square(n, part):
                pool.wait_ge(ffn_relu, 2 * n + part + 1)
                h = hid[:, part * BANK:(part + 1) * BANK]
                g_.tensor_tensor(h, h, h, ALU.mult).then_inc(ffn_sq, 1)

            def neuron(n, r, first, last):
                for k in range(first, last + 1):
                    step, part = divmod(k + 3, 5)
                    y_n = y[:, r, :]
                    last_mem, last_spk = (y_n, cnt[:, :]) if step == 1 else (mem[:, :], spk[:, :])
                    if k == 1:
                        stand_alone(pool, (ffn_ysb, n + 1), (ffn_out, n))
                        ins = g_.tensor_scalar(cnt[:, :], y_n, THRESHOLD, 0.0, ALU.is_gt, ALU.add)
                    else:
                        stand_alone(pool, (lif, LIF_OPS * n + k - 1))
                        if part == 0:
                            ins = g_.tensor_scalar(mem[:, :], last_mem, BETA, 0.0, ALU.mult, ALU.add)
                        elif part == 1:
                            ins = g_.tensor_tensor(mem[:, :], mem[:, :], y_n, ALU.add)
                        elif part == 2:
                            ins = g_.tensor_tensor(mem[:, :], mem[:, :], last_spk, ALU.subtract)
                        elif part == 3:
                            ins = g_.tensor_scalar(spk[:, :], mem[:, :], THRESHOLD, 0.0, ALU.is_gt, ALU.add)
                        else:
                            ins = g_.tensor_tensor(cnt[:, :], cnt[:, :], spk[:, :], ALU.add)
                    ins.then_inc(lif, 1)

            def spread(ap, m):
                return ap.unsqueeze(2).broadcast_to([P, ap.shape[1], m])

            def row_distance(i, par):
                pool.wait_ge(att_min, i + 1)
                g_.tensor_tensor(dlt[:, :, :], spread(nrow[:, :], NCH), nmax[:, par, :, :], ALU.subtract).then_inc(att_dlt, 1)

            def row_sums(i, par):
                pool.wait_ge(att_fac, i + 1)
                pool.wait_ge(exp_a, CPT * i + CPT)
                g_.tensor_tensor(sume[:, :, :], esum[:, par, :, :], fac[:, :, :], ALU.mult).then_inc(att_sum, 1)
                pool.wait_ge(att_sum, 2 * i + 1)
                g_.tensor_tensor(tot[:, :], sume[:, :, 0], sume[:, :, 1], ALU.add).then_inc(att_sum, 1)

            def row_output(i, par):
                pool.wait_ge(att_rec, i + 1)
                g_.tensor_tensor(wgt[:, :, :], sume[:, :, :], spread(rec[:, :], NCH), ALU.mult).then_inc(att_step, 1)
                pool.wait_ge(att_step, 2 * i + 1)
                g_.tensor_tensor(wsum[:, :], wgt[:, :, 0], wgt[:, :, 1], ALU.add).then_inc(att_step, 1)
                pool.wait_ge(att_step, 2 * i + 2)
                if isinstance(i, int):
                    pool.wait_ge(xv_loaded[par], 32 * (i // 2 + 1))
                else:
                    pool.wait_ge(xv_loaded[par], 16 * (i - par) + 32)
                need(pool, opt_tr, i)
                g_.tensor_tensor(opt.rearrange("p (h d) -> p h d", h=H), va[:, par, :].rearrange("p (h d) -> p h d", h=H),
                                 spread(wsum[:, :], DH), ALU.mult).then_inc(att_opt, 1)

            def split_kv(i):
                stand_alone(pool, (qkv_kvf, i + 1), (parts_stored, 16 * 2 * PARTS * i))
                g_.tensor_scalar(kvparts[:, 0, :], kvf, 1.0, 0.0, ALU.mult, ALU.add).then_inc(qkv_split, 1)
                pool.wait_ge(qkv_split, 4 * i + 1)
                g_.tensor_tensor(kvres, kvf, kvparts[:, 0, :], ALU.subtract).then_inc(qkv_split, 1)
                stand_alone(pool, (qkv_split, 4 * i + 2))
                g_.tensor_scalar(kvparts[:, 1, :], kvres, 1.0, 0.0, ALU.mult, ALU.add).then_inc(qkv_split, 1)
                pool.wait_ge(qkv_split, 4 * i + 3)
                g_.tensor_tensor(kvparts[:, 2, :], kvres, kvparts[:, 1, :], ALU.subtract).then_inc(qkv_split, 1)

            def phase_a(it, par, _):
                i1, i2, i3 = (tile_at(it, n) for n in (1, 2, 3))
                if i1 is not None:
                    row_distance(i1, 1 - par)
                if i3 is not None:
                    neuron(i3, 1 - par, 20, LIF_OPS)
                if i1 is not None:
                    row_sums(i1, 1 - par)
                if i2 is not None:
                    neuron(i2, par, 1, 1)
                if i1 is not None:
                    row_output(i1, 1 - par)
                if i3 is not None:
                    normalise(i3, 1, qkv_mv, qkv_step, xn2, xout[:, 1 - par, :], qkv_tr, i3).then_inc(qkv_xn, 1)
                if i2 is not None:
                    neuron(i2, par, 2, 5)
                if i1 is not None:
                    normalise(i1, 0, ffn_mv, ffn_step, xn[:, :], xin[:, 1 - par, :], ffn_tr, i1).then_inc(ffn_xn, 1)
                if i2 is not None:
                    neuron(i2, par, 6, 7)
                if i3 is not None:
                    split_kv(i3)
                if i1 is not None:
                    square(i1, 0)
                if i2 is not None:
                    neuron(i2, par, 8, 10)
                if i1 is not None:
                    square(i1, 1)
                if i2 is not None:
                    neuron(i2, par, 11, 19)
            iterations(pool, phase_a)

            def half_distance(i, par, half):
                n, t0 = 2 * i + half, HALF * half
                pool.wait_ge(w_min, n + 1)
                g_.tensor_tensor(dlt[:, 0:HALF, :], spread(nrow[:, 0:HALF], NCH), nmax[:, par, t0:t0 + HALF, :], ALU.subtract) \
                    .then_inc(w_dlt, 1)

            def half_sums(i, par, half):
                n, t0 = 2 * i + half, HALF * half
                pool.wait_ge(w_fac, n + 1)
                pool.wait_ge(exp_b, CPT * i + CPT // 2 * (half + 1))
                g_.tensor_tensor(sume[:, 0:HALF, :], esum[:, par, t0:t0 + HALF, :], fac[:, 0:HALF, :], ALU.mult).then_inc(w_sum, 1)
                pool.wait_ge(w_sum, 2 * n + 1)
                g_.tensor_tensor(tot[:, 0:HALF], sume[:, 0:HALF, 0], sume[:, 0:HALF, 1], ALU.add).then_inc(w_sum, 1)

            def weigh_q(i, par, half):
                n = 2 * i + half
                pool.wait_ge(w_rec, n + 1)
                g_.tensor_tensor(wgt[:, 0:HALF, :], fac[:, 0:HALF, :], spread(rec[:, 0:HALF], NCH), ALU.mult).then_inc(w_step, 1)
                pool.wait_ge(w_step, n + 1)
                need(pool, prod_ready, 4 * n)
                q = qcol[:, par, :].rearrange("p (m j r) -> p r m j", m=KC, r=8)
                for c in range(NCH):
                    last = g_.tensor_tensor(qw[:, c, :, 0:DH].rearrange("p (r m) j -> p r m j", m=KC),
                                            q[:, 4 * half:4 * half + 4, :, :],
                                            wgt[:, 0:HALF, c].rearrange("p (r m) -> p r m", m=KC).unsqueeze(3)
                                            .broadcast_to([P, 4, KC, DH]), ALU.mult)
                last.then_inc(w_qw, 1)

            def add_pieces(i, par):
                pool.wait_ge(x2_loaded, 16 * (i + 1))
                pool.wait_ge(pieces_loaded, 16 * 4 * (i + 1))
                need(pool, ffn_out, T + i - 1)
                for g in range(4):
                    src = x2_in[:, :] if g == 0 else xin[:, par, :]
                    ins = g_.tensor_tensor(xin[:, par, :], src, pieces[:, g, :], ALU.add)
                    if g < 3:
                        ins.then_inc(x3_step, 1)
                        pool.wait_ge(x3_step, 3 * i + g + 1)
                ins.then_inc(x3_ready, 1)

            def phase_b(it, par, _):
                i, i1, i2, i3 = (tile_at(it, n) for n in range(4))
                if i1 is not None:
                    half_sums(i1, 1 - par, 1)
                if i3 is not None:
                    neuron(T + i3, 1 - par, 9, 9)
                if i1 is not None:
                    weigh_q(i1, 1 - par, 1)
                if i3 is not None:
                    neuron(T + i3, 1 - par, 10, 11)
                if i2 is not None:
                    square(T + i2, 0)
                if i3 is not None:
                    neuron(T + i3, 1 - par, 12, 15)
                if i2 is not None:
                    square(T + i2, 1)
                if i3 is not None:
                    neuron(T + i3, 1 - par, 16, 19)
                if i is not None:
                    half_distance(i, par, 0)
                if i3 is not None:
                    neuron(T + i3, 1 - par, 20, 20)
                if i is not None:
                    half_sums(i, par, 0)
                if i3 is not None:
                    neuron(T + i3, 1 - par, 21, LIF_OPS)
                if i is not None:
                    weigh_q(i, par, 0)
                if i2 is not None:
                    neuron(T + i2, par, 1, 1)
                if i1 is not None:
                    add_pieces(i1, 1 - par)
                if i2 is not None:
                    neuron(T + i2, par, 2, 4)
                if i1 is not None:
                    normalise(T + i1, 0, ffn_mv, ffn_step, xn[:, :], xin[:, 1 - par, :], ffn_tr, T + i1).then_inc(ffn_xn, 1)
                if i2 is not None:
                    neuron(T + i2, par, 5, 8)
                if i is not None:
                    half_distance(i, par, 1)
            iterations(pool, phase_b)


_NAMES = ["x", "w_in", "b_in_col", "b_in_row", "w_out", "b_out", "wq", "bq_col", "wkv", "bkv_row", "temp", "w_fc", "w_proj"]


def kernel(**inputs):
    import numpy as np
    import concourse.bacc as bacc
    from concourse.bass_utils import run_bass_kernel_spmd as run

    a = {n: np.asarray(v) for n, v in inputs.items()}
    w_in = a["L0_attn_a_w_in"].reshape(H, 3, DH, D).transpose(1, 0, 2, 3).reshape(3 * D, D)
    b_in = a["L0_attn_a_b_in"].reshape(H, 3, DH).transpose(1, 0, 2).reshape(3 * D)
    laid = {
        "x": a["L0_attn_a_x"].reshape(TOK, D),
        "w_in": w_in.T,
        "b_in_col": b_in[:2 * D].reshape(2 * KC, P).T,
        "b_in_row": b_in[2 * D:].reshape(1, D),
        "w_out": a["L0_attn_a_w_out"].T,
        "b_out": a["L0_attn_a_b_out"].reshape(1, D),
        "wq": a["L0_attn_b_Wq"],
        "bq_col": a["L0_attn_b_bq"].reshape(KC, P).T,
        "wkv": np.concatenate([a["L0_attn_b_Wk"], a["L0_attn_b_Wv"]], axis=1),
        "bkv_row": np.concatenate([a["L0_attn_b_bk"], a["L0_attn_b_bv"]]).reshape(1, 2 * D),
        "temp": a["L0_attn_b_temperature"].reshape(1, H),
        "w_fc": a["L0_ffn_W_fc"].T,
        "w_proj": a["L0_ffn_W_proj"].T,
    }
    nc = bacc.Bacc("TRN2", target_bir_lowering=False, num_devices=1)
    arrays, args = {}, []
    for name in _NAMES:
        arrays["in_" + name] = np.ascontiguousarray(laid[name])
        args.append(nc.dram_tensor("in_" + name, arrays["in_" + name].shape, FP32, kind="ExternalInput").ap())
    out = nc.dram_tensor("out", (BATCH, SEQ, D), FP32, kind="ExternalOutput").ap()
    build(nc, *args, out.rearrange("b l d -> (b l) d"))
    r = run(nc, [arrays], core_ids=[0])
    return r.results[0]["out"]
```

```python
from contextlib import ExitStack

import concourse.bass as bass
from concourse import mybir

FP32 = mybir.dt.float32
BF16 = mybir.dt.bfloat16
ALU = mybir.AluOpType
ACT = mybir.ActivationFunctionType
AX = mybir.AxisListType

P = 128
BATCH, SEQ, D = 2, 2048, 256
H, DH = 16, 16
FF = 1024
KC = D // P
TOK = BATCH * SEQ
T = TOK // P
TPB = SEQ // P
GROUP = 512
NG = TOK // GROUP
SUB = GROUP // P
EARLY_HEADS = 12
BANK = 512
CH = 1024
NCH = SEQ // CH
CPT = H * NCH
NBUF = 3
HALF = H // 2
EPS = 1e-5
BETA, THRESHOLD, STEPS = 0.9, 1.0, 5
PARTS = 3
Q_SLOTS = [0, 0, 0, 1, 1, 1, 2, 2]
K_SLOTS = [0, 1, 2, 0, 1, 2, 0, 1]
TURN_A, TURN_B = 7, 8
DRAIN = 3
LIF_OPS = 1 + 5 * (STEPS - 1)
N_PRELUDE_LOADS, N_WEIGHT_LOADS = 5, 8
KV_A, Q_A = [13, 14, 15, 16], [18, 20]
UP_A, UP_B = [18, 19, 20, 21, 22, 23, 24, 25], [4, 4, 5, 5, 8, 11, 14, 14]
DOWN_A, DOWN_B = [26, 26, 27, 27, 28, 29, 30, 30], [17, 18, 18, 19, 19, 20, 20, 21]
PROD_AT = [6, 7, 9, 10, 12, 13, 15, 16], [22, 23, 25, 26, 28, 29, 31, 32]


def build(nc, x, w_in, b_in_col, b_in_row, w_out, b_out, wq, bq_col, wkv, bkv_row, temp, w_fc, w_proj, out):
    q_parts = nc.dram_tensor("q_parts", (PARTS, D, TOK), BF16).ap()
    k_parts = nc.dram_tensor("k_parts", (PARTS, D, TOK), BF16).ap()
    v_rows = nc.dram_tensor("v_rows", (TOK, D), FP32).ap()
    x2_rows = nc.dram_tensor("x2_rows", (TOK, D), FP32).ap()
    kb_parts = nc.dram_tensor("kb_parts", (PARTS, TOK, D), BF16).ap()
    vb_parts = nc.dram_tensor("vb_parts", (PARTS, TOK, D), BF16).ap()
    qb_cols = nc.dram_tensor("qb_cols", (T * P, D), FP32).ap()

    ctx = ExitStack()
    with ctx:
        def sb(name, shape, dt=FP32):
            return ctx.enter_context(nc.sbuf_tensor(name, shape, dt))

        def pb(name, shape):
            return ctx.enter_context(nc.psum_tensor(name, shape, FP32))

        def sem(name):
            return ctx.enter_context(nc.semaphore(name))

        big = sb("big", [P, H * SEQ])
        keys = big[:, :].bitcast(BF16).rearrange("p (b h m) -> p b h m", b=BATCH, h=H)
        expo = big[:, :].rearrange("p (t s) -> p t s", t=H)
        at = EARLY_HEADS * SEQ // 2

        def carve(n):
            nonlocal at
            at += n
            return big[:, at - n:at]
        px = [carve(SUB * D).rearrange("p (s d) -> p s d", s=SUB) for _ in range(2)]
        pxn = carve(SUB * D).rearrange("p (s d) -> p s d", s=SUB)
        pxT = carve(KC * GROUP).rearrange("p (k n) -> p k n", k=KC)
        pqk = carve(2 * KC * GROUP).rearrange("p (m n) -> p m n", m=2 * KC)
        pres = carve(2 * KC * GROUP).rearrange("p (m n) -> p m n", m=2 * KC)
        pparts = [carve(PARTS * KC * GROUP).bitcast(BF16).rearrange("p (a m n) -> p a m n", a=PARTS, m=2 * KC) for _ in range(2)]
        pv_sb = carve(SUB * D).rearrange("p (s d) -> p s d", s=SUB)
        pstat = carve(SUB * 6).rearrange("p (s k) -> p s k", s=SUB)
        pmv = carve(SUB * 2).rearrange("p (s k) -> p s k", s=SUB)
        prstd = carve(SUB)
        pvar = carve(SUB)
        bias_res = carve(4 * D)[0:1, :]
        bias_parts = [carve(2 * D)[0:1, :].bitcast(BF16) for _ in range(PARTS)]
        w_in_sb = carve(KC * 3 * D).rearrange("p (k n) -> p k n", k=KC)


        w_out_sb = sb("w_out_sb", [P, KC, D])
        wq_sb = sb("wq_sb", [P, KC, D])
        wkv_sb = sb("wkv_sb", [P, KC, 2 * D])
        w_fc_sb = sb("w_fc_sb", [P, KC, FF])
        w_proj_sb = sb("w_proj_sb", [P, FF // P, D])
        bin_col = sb("bin_col", [P, 2 * KC])
        bq_scaled = sb("bq_scaled", [P, KC])
        bqb_col = sb("bqb_col", [P, KC])
        temp_sb = sb("temp_sb", [P, T])
        ident = sb("ident", [P, P])
        ones = sb("ones", [PARTS, P], BF16)
        bias = sb("bias", [PARTS, 4 * D], BF16)
        power = sb("power", [P, SUB])

        shared = sb("shared", [P, 4 * SEQ // 2])
        qstack = shared[:, 0:2 * H * P // 2].bitcast(BF16).rearrange("p (r h n) -> p r h n", r=2, h=H)
        kvf = shared[:, 2048:2560]
        kvres = shared[:, 2560:3072]
        kvparts = shared[:, 3072:3840].bitcast(BF16).rearrange("p (a n) -> p a n", a=PARTS)
        bstack = shared[:, :].bitcast(BF16).rearrange("p (r a n) -> p r a n", r=2, a=2)
        shared2 = sb("shared2", [P, SEQ])
        xa = shared2[:, 0:512].rearrange("p (r d) -> p r d", r=2)
        va = shared2[:, 512:1024].rearrange("p (r d) -> p r d", r=2)
        opt = shared2[:, 1024:1280]
        optT = shared2[:, 1280:1536].rearrange("p (k n) -> p k n", k=KC)
        prod = shared2[:, :]

        qcol = sb("qcol", [P, 2, D])
        pieces = sb("pieces", [P, 4, D])
        row_bias = pieces[0:1, :, :].rearrange("o a d -> o (a d)")
        xn2 = pieces[:, 0, :]
        xn2T = pieces[:, 1, :].rearrange("p (k n) -> p k n", k=KC)
        x2_in = sb("x2_in", [P, D])
        qw = sb("qw", [P, NCH, HALF, 2 * DH])
        xin = sb("xin", [P, 2, D])
        xout = sb("xout", [P, 2, D])
        xn = sb("xn", [P, D])
        xnT = sb("xnT", [P, KC, P])
        hid = sb("hid", [P, FF])
        y = sb("y", [P, 2, D])
        mem = sb("mem", [P, D])
        spk = sb("spk", [P, D])
        cnt = sb("cnt", [P, D])
        nmax = sb("nmax", [P, 2, H, NCH])
        esum = sb("esum", [P, 2, H, NCH])
        nrow = sb("nrow", [P, H])
        dlt = sb("dlt", [P, H, NCH])
        fac = sb("fac", [P, H, NCH])
        sume = sb("sume", [P, H, NCH])
        tot = sb("tot", [P, H])
        rec = sb("rec", [P, H])
        wgt = sb("wgt", [P, H, NCH])
        wsum = sb("wsum", [P, H])
        st = sb("st", [P, 2, 6])
        mv = sb("mv", [P, 2, 2])
        var = sb("var", [P, 2])
        rstd = sb("rstd", [P, 2])

        score = [pb(f"score{n}", [P, CH]) for n in range(NBUF)]
        bank_f = pb("bank_f", [P, BANK])
        bank_g = pb("bank_g", [P, BANK])

        w_in_loaded, bias_split, bias_loaded = sem("w_in_loaded"), sem("bias_split"), sem("bias_loaded")
        att_step, ffn_step, qkv_step, w_step = (sem(n) for n in ("att_step", "ffn_step", "qkv_step", "w_step"))
        w_loaded, consts, ident0, bq_ready = sem("w_loaded"), sem("consts"), sem("ident0"), sem("bq_ready")
        p_stats, p_aggr, p_rstd, p_xn = (sem(n) for n in ("p_stats", "p_aggr", "p_rstd", "p_xn"))
        p_tr, p_xT, p_qk, p_qkf, p_v, p_vs = (sem(n) for n in ("p_tr", "p_xT", "p_qk", "p_qkf", "p_v", "p_vs"))
        p_split, v_stored = sem("p_split"), sem("v_stored")
        px_loaded, qk_stored = ([sem(f"{n}{r}") for r in range(2)] for n in ("px_loaded", "qk_stored"))
        early_keys = sem("early_keys")
        keys_loaded = [sem(f"keys_loaded{b}") for b in range(BATCH)]
        q_loaded = [sem(f"q_loaded{r}") for r in range(2)]
        xv_loaded = [sem(f"xv_loaded{r}") for r in range(2)]
        scores_a, max_a, exp_a = sem("scores_a"), sem("max_a"), sem("exp_a")
        att_min, att_dlt, att_fac, att_sum, att_rec, att_opt = (
            sem(n) for n in ("att_min", "att_dlt", "att_fac", "att_sum", "att_rec", "att_opt"))
        opt_tr, opt_T, oproj = sem("opt_tr"), sem("opt_T"), sem("oproj")
        ffn_x1 = sem("ffn_x1")
        ffn_stats, ffn_mv, ffn_xn, ffn_tr, ffn_xT = (sem(n) for n in ("ffn_stats", "ffn_mv", "ffn_xn", "ffn_tr", "ffn_xT"))
        ffn_fc, ffn_relu, ffn_sq, ffn_y, ffn_ysb = (sem(n) for n in ("ffn_fc", "ffn_relu", "ffn_sq", "ffn_y", "ffn_ysb"))
        lif, ffn_out = sem("lif"), sem("ffn_out")
        qkv_stats, qkv_mv, qkv_xn, qkv_tr, qkv_xT = (sem(n) for n in ("qkv_stats", "qkv_mv", "qkv_xn", "qkv_tr", "qkv_xT"))
        qkv_kv, qkv_kvf, qkv_q, qkv_qf, qkv_split = (sem(n) for n in ("qkv_kv", "qkv_kvf", "qkv_q", "qkv_qf", "qkv_split"))
        parts_stored = sem("parts_stored")
        x2_stored, qb_stored = ([sem(f"{n}{r}") for r in range(2)] for n in ("x2_stored", "qb_stored"))
        b_loaded = [sem(f"b_loaded{r}") for r in range(2)]
        x2_loaded = sem("x2_loaded")
        scores_b, max_b, exp_b = sem("scores_b"), sem("max_b"), sem("exp_b")
        w_min, w_dlt, w_fac, w_sum, w_rec, w_qw = (sem(n) for n in ("w_min", "w_dlt", "w_fac", "w_sum", "w_rec", "w_qw"))
        prod_ready, prod_kept, prod_added = sem("prod_ready"), sem("prod_kept"), sem("prod_added")
        pieces_loaded, x3_step, x3_ready = sem("pieces_loaded"), sem("x3_step"), sem("x3_ready")
        out_stored = [sem(f"out_stored{r}") for r in range(2)]

        block = ctx.enter_context(nc.Block())

        def need(eng, s, value):
            if not (isinstance(value, int) and value <= 0):
                eng.wait_ge(s, value)

        def stand_alone(eng, *waits):
            waits = [(s, n if isinstance(n, int) else eng.to_reg(n)) for s, n in waits]
            eng.wait_ge(consts, 4)
            for s, n in waits:
                need(eng, s, n)

        def tile_at(it, lag):
            if isinstance(it, int) and not 0 <= it - lag < T:
                return None
            return it - lag

        def head0(it):
            return isinstance(it, int) and it == T

        def last_tile(n):
            return isinstance(n, int) and n in (T - 1, 2 * T - 1)

        def attention_q(i, r):
            return x2_in[:, :] if isinstance(i, int) and i == T - 2 else qcol[:, r, :]

        def neuron(eng, ops, n, r, first, last):
            for k in range(first, last + 1):
                step, part = divmod(k + 3, 5)
                y_n = y[:, r, :]
                last_mem, last_spk = (y_n, cnt[:, :]) if step == 1 else (mem[:, :], spk[:, :])
                if k == 1:
                    stand_alone(eng, (ffn_ysb, n + 1), (ffn_out, n))
                    ins = ops.tensor_scalar(cnt[:, :], y_n, THRESHOLD, 0.0, ALU.is_gt, ALU.add)
                else:
                    stand_alone(eng, (lif, LIF_OPS * n + k - 1))
                    if part == 0:
                        ins = ops.tensor_scalar(mem[:, :], last_mem, BETA, 0.0, ALU.mult, ALU.add)
                    elif part == 1:
                        ins = ops.tensor_tensor(mem[:, :], mem[:, :], y_n, ALU.add)
                    elif part == 2:
                        ins = ops.tensor_tensor(mem[:, :], mem[:, :], last_spk, ALU.subtract)
                    elif part == 3:
                        ins = ops.tensor_scalar(spk[:, :], mem[:, :], THRESHOLD, 0.0, ALU.is_gt, ALU.add)
                    else:
                        ins = ops.tensor_tensor(cnt[:, :], cnt[:, :], spk[:, :], ALU.add)
                ins.then_inc(lif, 1)

        def iterations(eng, body, cuts=(T,), first=0):
            for it in range(first, 6):
                body(it, it % 2, 0)
            low = 6
            for n, cut in enumerate(cuts):
                with eng.Fori(low, cut, 2) as it:
                    body(it, 0, n)
                    body(it + 1, 1, n)
                low = cut
            for it in range(low, T + DRAIN):
                body(it, it % 2, len(cuts) - 1)

        def buffers(turn):
            order = [0]
            for q in range(1, 2 * CPT):
                order.append((order[-1] + (1 if turn <= q < turn + CPT else -1)) % NBUF)
            return [(order[q], next(d for d in range(1, 2 * CPT) if order[q - d] == order[q])) for q in range(2 * CPT)]
        buffers_a, buffers_b = buffers(TURN_A), buffers(TURN_B)

        @block.sync
        def _(sp):
            loads = [
                (row_bias[:, 0:D], b_in_row),
                (row_bias[:, D:2 * D], b_out),
                (row_bias[:, 2 * D:4 * D], bkv_row),
                (w_in_sb, w_in.rearrange("(k p) n -> p k n", p=P)),
                (bin_col[:, :], b_in_col),
                (w_out_sb[:, :, :], w_out.rearrange("(k p) n -> p k n", p=P)),
                (wq_sb[:, :, :], wq.rearrange("(k p) n -> p k n", p=P)),
                (bqb_col[:, :], bq_col),
                (wkv_sb[:, :, :], wkv.rearrange("(k p) n -> p k n", p=P)),
                (temp_sb[:, 0:H], temp.broadcast_to([P, H])),
                (temp_sb[:, H:2 * H], temp.broadcast_to([P, H])),
                (w_fc_sb[:, :, :], w_fc.rearrange("(k p) n -> p k n", p=P)),
                (w_proj_sb[:, :, :], w_proj.rearrange("(k p) n -> p k n", p=P)),
            ]
            assert len(loads) == N_PRELUDE_LOADS + N_WEIGHT_LOADS

            def load_x(g, r):
                sp.dma_start(px[r], x[bass.ds(g * GROUP, GROUP), :].rearrange("(s p) d -> p s d", p=P)).then_inc(px_loaded[r], 16)

            def store_group(g, r):
                cols = bass.ds(g * GROUP, GROUP)
                stand_alone(sp, (p_vs, g + 1))
                sp.dma_start(v_rows[cols, :].rearrange("(s p) d -> p s d", p=P), pv_sb).then_inc(v_stored, 16)
                stand_alone(sp, (p_split, 4 * g + 4))
                for a in range(PARTS):
                    for dst, part in ((q_parts, slice(0, KC)), (k_parts, slice(KC, 2 * KC))):
                        sp.dma_start(dst[a, :, cols].rearrange("(m p) n -> p m n", p=P), pparts[r][:, a, part, :]) \
                          .then_inc(qk_stored[r], 16)

            def load_store(g, r):
                stand_alone(sp, (p_xn, g + 1))
                load_x(g + 2, r)
                store_group(g, r)

            def load_keys(b, h0, h1, done):
                for n in range(8):
                    src = k_parts[K_SLOTS[n], h0 * DH:h1 * DH, b * SEQ:(b + 1) * SEQ].rearrange("(h d) m -> d h m", d=DH)
                    sp.dma_start(keys[n * DH:(n + 1) * DH, b, h0:h1, :], src).then_inc(done, 16)

            def load_q(i, par):
                for n in range(8):
                    src = q_parts[Q_SLOTS[n], :, bass.ds(i * P, P)].rearrange("(h d) n -> d h n", d=DH)
                    sp.dma_start(qstack[n * DH:(n + 1) * DH, par, :, :], src).then_inc(q_loaded[par], 16)

            load_x(0, 0)
            load_x(1, 1)
            for n, (dst, src) in enumerate(loads):
                sp.dma_start(dst, src).then_inc(w_in_loaded if n < N_PRELUDE_LOADS else w_loaded, 16)
            sp.wait_ge(bias_split, 4)
            for a in range(PARTS):
                sp.dma_start(bias[a:a + 1, :], bias_parts[a]).then_inc(bias_loaded, 16)
            with sp.Fori(0, NG // 2, 2) as g:
                load_store(g, 0)
                load_store(g + 1, 1)
            load_store(NG // 2, 0)
            for r in range(2):
                sp.wait_ge(qk_stored[r], 16 * 2 * PARTS * NG // 4)
            load_q(0, 0)
            for n, g in enumerate(range(NG // 2 + 1, NG)):
                load_keys(0, n * EARLY_HEADS // 3, (n + 1) * EARLY_HEADS // 3, early_keys)
                if g < NG - 2:
                    load_store(g, g % 2)
                else:
                    store_group(g, g % 2)

            sp.wait_ge(p_qk, 4 * NG)
            sp.wait_ge(p_v, NG)
            sp.wait_ge(v_stored, 16 * NG)
            for r in range(2):
                sp.wait_ge(qk_stored[r], 16 * 2 * PARTS * NG // 2)
            load_keys(0, EARLY_HEADS, H, keys_loaded[0])
            load_keys(1, 0, H, keys_loaded[1])

            def load_b_side(i, par, side):
                parts, slots = ((kb_parts, Q_SLOTS), (vb_parts, K_SLOTS))[side]
                for n in range(8):
                    src = parts[slots[n], bass.ds(i * P, P), :].rearrange("(r j) d -> r (j d)", r=DH)
                    sp.dma_start(bstack[n * DH:(n + 1) * DH, par, side, :], src).then_inc(b_loaded[par], 16)

            def load_b_q(i, par):
                sp.dma_start(qcol[:, par, :], qb_cols[bass.ds(i * P, P), :]).then_inc(b_loaded[par], 16)

            def phase_a(it, par, _):
                if head0(it + 1):
                    sp.wait_ge(scores_a, CPT * (T - 1))
                    sp.wait_ge(parts_stored, 16 * 2 * PARTS)
                    load_b_side(0, 0, 0)
                if head0(it):
                    sp.wait_ge(scores_a, CPT * T)
                    for r in range(2):
                        sp.wait_ge(qb_stored[r], 16 * (T // 2 - 1 - r))
                    load_b_side(0, 0, 1)
                    load_b_q(0, 0)
                i = tile_at(it, 0)
                if i is not None:
                    if not (isinstance(i, int) and i == T - 1):
                        stand_alone(sp, (scores_a, CPT * i))
                        load_q(i + 1, 1 - par)
                    stand_alone(sp, (att_opt, i - 1), (ffn_x1, i - 1))
                    sp.dma_start(xa[:, par, :], x[bass.ds(i * P, P), :]).then_inc(xv_loaded[par], 16)
                    sp.dma_start(va[:, par, :], v_rows[bass.ds(i * P, P), :]).then_inc(xv_loaded[par], 16)
                i = tile_at(it, 3)
                if i is not None:
                    r = (par + 1) % 2
                    row = bass.ds(i * P, P)
                    stand_alone(sp, (ffn_out, i + 1))
                    sp.dma_start(x2_rows[row, :], xout[:, r, :]).then_inc(x2_stored[r], 16)
                    stand_alone(sp, (qkv_qf, i + 1))
                    sp.dma_start(qb_cols[row, :], attention_q(i, r)).then_inc(qb_stored[r], 16)
                    stand_alone(sp, (qkv_split, 4 * i + 4))
                    for a in range(PARTS):
                        sp.dma_start(kb_parts[a, row, :], kvparts[:, a, 0:D]).then_inc(parts_stored, 16)
                        sp.dma_start(vb_parts[a, row, :], kvparts[:, a, D:2 * D]).then_inc(parts_stored, 16)
            iterations(sp, phase_a, (T - 2,))

            for r in range(2):
                sp.wait_ge(x2_stored[r], 16 * T // 2)
                sp.wait_ge(qb_stored[r], 16 * T // 2)
            sp.wait_ge(parts_stored, 16 * 2 * PARTS * T)


            def phase_b(it, par, _):
                i = tile_at(it, 0)
                if i is not None and not (isinstance(i, int) and i == T - 1):
                    stand_alone(sp, (scores_b, CPT * i), (w_qw, 2 * i))
                    load_b_side(i + 1, 1 - par, 0)
                    load_b_side(i + 1, 1 - par, 1)
                    load_b_q(i + 1, 1 - par)
                i = tile_at(it, 1)
                if i is not None:
                    stand_alone(sp, (x3_ready, i))
                    sp.dma_start(x2_in[:, :], x2_rows[bass.ds(i * P, P), :]).then_inc(x2_loaded, 16)
                    stand_alone(sp, (prod_added, 4 * i + 4))
                    for g in range(4):
                        sp.dma_start(pieces[:, g, :], prod[32 * g:32 * g + DH, :].rearrange("r (j d) -> r j d", j=8)) \
                          .then_inc(pieces_loaded, 16)
                i = tile_at(it, 3)
                if i is not None:
                    r = (par + 1) % 2
                    stand_alone(sp, (ffn_out, T + i + 1))
                    sp.dma_start(out[bass.ds(i * P, P), :], xout[:, r, :]).then_inc(out_stored[r], 16)
            iterations(sp, phase_b, (T - 2,))
            for r in range(2):
                sp.wait_ge(out_stored[r], 16 * T // 2)

        @block.tensor
        def _(pe):
            mm = nc.tensor.matmul

            def transpose2(dst, src):
                for k in range(KC):
                    last = nc.tensor.transpose(dst[:, k * P:(k + 1) * P], src[:, k * P:(k + 1) * P], ident[:, :])
                return last

            pe.wait_ge(w_in_loaded, 16 * N_PRELUDE_LOADS)
            pe.wait_ge(consts, 4)
            pe.wait_ge(bias_loaded, 16 * PARTS)

            def tr(g):
                pe.wait_ge(p_xn, g + 1)
                need(pe, p_xT, g)
                for k in range(KC):
                    for s in range(SUB):
                        last = nc.tensor.transpose(score[0][:, k * GROUP + s * P:k * GROUP + (s + 1) * P],
                                                   pxn[:, s, k * P:(k + 1) * P], ident[:, :])
                last.then_inc(p_tr, 1)

            def project(g):
                pe.wait_ge(p_xT, g + 1)
                need(pe, p_qkf, g)
                for m in range(2 * KC):
                    dst = score[1 + m // 2][:, (m % 2) * GROUP:(m % 2 + 1) * GROUP]
                    for k in range(KC):
                        last = mm(dst, w_in_sb[:, k, m * P:(m + 1) * P], pxT[:, k, :], start=(k == 0), stop=(k == KC - 1))
                    last.then_inc(p_qk, 1)
                need(pe, p_vs, g)
                for s in range(SUB):
                    dst = (bank_f, bank_g)[s // 2][:, (s % 2) * D:(s % 2 + 1) * D]
                    for k in range(KC):
                        mm(dst, pxT[:, k, s * P:(s + 1) * P], w_in_sb[:, k, 2 * D:3 * D], start=(k == 0), stop=False)
                    last = mm(dst, ones[:, :], bias[:, 0:D], start=False, stop=True)
                last.then_inc(p_v, 1)
            tr(0)
            project(0)
            with pe.Fori(1, NG) as g:
                tr(g)
                project(g)
            pe.wait_ge(p_qkf, NG)
            pe.wait_ge(p_vs, NG)
            pe.wait_ge(w_loaded, 16 * N_WEIGHT_LOADS)

            def ffn_transpose(n):
                pe.wait_ge(ffn_xn, n + 1)
                need(pe, ffn_ysb, n)
                transpose2(bank_f, xn).then_inc(ffn_tr, 1)

            def ffn_up(n, f):
                if f == 0:
                    pe.wait_ge(ffn_xT, n + 1)
                if f == 4:
                    pe.wait_ge(ffn_relu, 2 * n + 1)
                for k in range(KC):
                    last = mm(bank_f[:, (f % 4) * P:(f % 4 + 1) * P], w_fc_sb[:, k, f * P:(f + 1) * P], xnT[:, k, :],
                              start=(k == 0), stop=(k == KC - 1))
                if f % 4 == 3:
                    last.then_inc(ffn_fc, 1)

            def ffn_down(n, f):
                if f == 0:
                    pe.wait_ge(ffn_relu, 2 * n + 2)
                if f % 4 == 0:
                    pe.wait_ge(ffn_sq, 2 * n + f // 4 + 1)
                last = mm(bank_f[:, 0:D], hid[:, f * P:(f + 1) * P], w_proj_sb[:, f, :], start=(f == 0), stop=(f == FF // P - 1))
                if f == FF // P - 1:
                    last.then_inc(ffn_y, 1)

            def product(i, half, sc, rr):
                if rr == 0:
                    if sc == 0:
                        pe.wait_ge(w_qw, 2 * i + half + 1)
                    if half == 0:
                        need(pe, prod_kept, 4 * i + sc)
                        if sc == 0:
                            need(pe, prod_added, 4 * i)
                            if isinstance(i, int) and i == 0:
                                pe.wait_ge(qkv_qf, T - 2)
                    else:
                        pe.wait_ge(prod_kept, 4 * i + 4)
                        if sc == 0 and isinstance(i, int) and i == 0:
                            pe.wait_ge(qkv_qf, T)
                        need(pe, prod_added, 4 * i + sc)
                for g in range(4):
                    n = 4 * rr + g
                    last = mm(bank_g[32 * g:32 * g + 32, :], qw[:, sc * BANK // CH, n, :],
                              expo[:, HALF * half + n, sc * BANK:(sc + 1) * BANK], start=(rr == 0), stop=(rr == 1))
                if rr == 1:
                    last.then_inc(prod_ready, 1)

            def head_scores(i, par, c):
                if c == 0:
                    if isinstance(i, int):
                        pe.wait_ge(b_loaded[par], 16 * 17 * (i // 2 + 1))
                    else:
                        pe.wait_ge(b_loaded[par], 8 * 17 * (i - par) + 16 * 17)
                buf, ago = buffers_b[CPT * par + c]
                if isinstance(i, int) and i == 0 and c < ago:
                    last = max(q for q in range(2 * CPT) if buffers_a[q][0] == buf)
                    pe.wait_ge(exp_a, CPT * (T - 2) + last + 1)
                need(pe, exp_b, CPT * i + c - ago + 1)
                row = c // NCH * P
                for k in range(CH // BANK):
                    col = (c % NCH) * CH + k * BANK
                    last = mm(score[buf][:, k * BANK:(k + 1) * BANK], bstack[:, par, 0, row:row + P],
                              bstack[:, par, 1, col:col + BANK], start=True, stop=True)
                last.then_inc(scores_b, 1)

            def head_product(i, c):
                for n, at_c in enumerate(PROD_AT[1]):
                    if c == (min(at_c, CPT - 1) if isinstance(i, int) and i == 0 else at_c):
                        product(i, 0, n // 2, n % 2)

            def phase_a(it, par, b):
                i, i1, i3 = tile_at(it, 0), tile_at(it, 1), tile_at(it, 3)
                if isinstance(it, int):
                    b = min(it, T - 1) // TPB
                if i is not None:
                    if isinstance(i, int):
                        pe.wait_ge(q_loaded[par], 128 * (i // 2 + 1))
                    else:
                        pe.wait_ge(q_loaded[par], 64 * (i - par) + 128)
                    if b == 0:
                        pe.wait_ge(early_keys, 3 * 128)
                    else:
                        pe.wait_ge(keys_loaded[1], 128)
                for c in range(CPT):
                    if i is not None:
                        if c == EARLY_HEADS * NCH and b == 0:
                            pe.wait_ge(keys_loaded[0], 128)
                        buf, ago = buffers_a[CPT * par + c]
                        need(pe, exp_a, CPT * i + c - ago + 1)
                        for k in range(CH // BANK):
                            col = (c % NCH) * CH + k * BANK
                            last = mm(score[buf][:, k * BANK:(k + 1) * BANK], qstack[:, par, c // NCH, :],
                                      keys[:, b, c // NCH, col:col + BANK], start=True, stop=True)
                        last.then_inc(scores_a, 1)
                    elif head0(it):
                        head_scores(0, 0, c)
                    if i3 is not None:
                        if c == 12:
                            pe.wait_ge(qkv_xn, i3 + 1)
                            if isinstance(i3, int) and i3 >= T - 2:
                                pe.wait_ge(prod_kept, 4)
                            need(pe, qkv_qf, i3)
                            transpose2(bank_g, xn2).then_inc(qkv_tr, 1)
                        for n in range(2 * KC):
                            if c == KV_A[n]:
                                side, k = divmod(n, KC)
                                cols = slice(side * D, (side + 1) * D)
                                if n == 0:
                                    pe.wait_ge(qkv_xT, i3 + 1)
                                last = mm(bank_g[:, cols], xn2T[:, k, :], wkv_sb[:, k, cols], start=(k == 0), stop=False)
                                if k == KC - 1:
                                    last = mm(bank_g[:, cols], ones[:, :], bias[:, 2 * D + side * D:3 * D + side * D],
                                              start=False, stop=True)
                                    if side == 1:
                                        last.then_inc(qkv_kv, 1)
                        for m in range(KC):
                            if c == Q_A[m]:
                                if m == 0:
                                    pe.wait_ge(qkv_kvf, i3 + 1)
                                for k in range(KC):
                                    last = mm(bank_g[:, m * P:(m + 1) * P], wq_sb[:, k, m * P:(m + 1) * P], xn2T[:, k, :],
                                              start=(k == 0), stop=(k == KC - 1))
                                if m == KC - 1:
                                    last.then_inc(qkv_q, 1)
                    if i1 is not None:
                        if c == 9:
                            pe.wait_ge(att_opt, i1 + 1)
                            need(pe, ffn_ysb, i1)
                            transpose2(bank_f, opt).then_inc(opt_tr, 1)
                        if c in (10, 11):
                            k = c - 10
                            if k == 0:
                                pe.wait_ge(opt_T, i1 + 1)
                            last = mm(bank_f[:, D:2 * D], optT[:, k, :], w_out_sb[:, k, :], start=(k == 0), stop=False)
                            if k == KC - 1:
                                mm(bank_f[:, D:2 * D], ones[:, :], bias[:, D:2 * D], start=False, stop=True).then_inc(oproj, 1)
                        if c == 17:
                            ffn_transpose(i1)
                        for f in range(FF // P):
                            if c == UP_A[f]:
                                ffn_up(i1, f)
                        for f in range(FF // P):
                            if c == DOWN_A[f]:
                                ffn_down(i1, f)
                    if head0(it):
                        head_product(0, c)
            iterations(pe, phase_a, (TPB, T))

            def phase_b(it, par, _):
                i, i1, i2 = tile_at(it, 0), tile_at(it, 1), tile_at(it, 2)
                for c in range(CPT):
                    if i is not None:
                        head_scores(i, par, c)
                    if i2 is not None:
                        if c == 1:
                            ffn_transpose(T + i2)
                        for f in range(FF // P):
                            if c == UP_B[f]:
                                ffn_up(T + i2, f)
                        for f in range(FF // P):
                            if c == DOWN_B[f]:
                                ffn_down(T + i2, f)
                    if i1 is not None and c + CPT in PROD_AT[1] and not (isinstance(i1, int) and i1 == 0):
                        product(i1, 0, 3, 1)
                    if i1 is not None and c in PROD_AT[0]:
                        n = PROD_AT[0].index(c)
                        product(i1, 1, n // 2, n % 2)
                    if i is not None:
                        head_product(i, c)
            iterations(pe, phase_b, first=1)

        @block.vector
        def _(dve):
            v = nc.vector
            v.memset(ones[:, :], 1.0).then_inc(consts, 1)
            v.memset(power[:, :], -0.5).then_inc(consts, 1)
            v.memset(qw[:, :, :, :], 0.0).then_inc(consts, 1)
            dve.wait_ge(w_in_loaded, 16 * N_PRELUDE_LOADS)
            v.tensor_scalar(bq_scaled[:, :], bin_col[:, 0:KC], DH ** -0.5, None, ALU.mult).then_inc(bq_ready, 1)
            v.tensor_copy(bias_parts[0], row_bias).then_inc(bias_split, 1)
            dve.wait_ge(bias_split, 1)
            v.tensor_tensor(bias_res, row_bias, bias_parts[0], ALU.subtract).then_inc(bias_split, 1)
            dve.wait_ge(bias_split, 2)
            v.tensor_copy(bias_parts[1], bias_res).then_inc(bias_split, 1)
            dve.wait_ge(bias_split, 3)
            v.tensor_tensor(bias_parts[2], bias_res, bias_parts[1], ALU.subtract).then_inc(bias_split, 1)

            def norm(g, r):
                if isinstance(g, int):
                    dve.wait_ge(px_loaded[r], 16 * (g // 2 + 1))
                else:
                    dve.wait_ge(px_loaded[r], 8 * (g - r) + 16)
                for s in range(SUB):
                    v.bn_stats(pstat[:, s, :], px[r][:, s, :]).then_inc(p_stats, 1)
                need(dve, p_rstd, 2 * g)
                for s in range(SUB):
                    stand_alone(dve, (p_stats, SUB * g + s + 1))
                    v.bn_aggr(pmv[:, s, :], pstat[:, s, :]).then_inc(p_aggr, 1)
                dve.wait_ge(p_rstd, 2 * g + 2)
                need(dve, p_tr, g)
                dve.wait_ge(p_aggr, SUB * g + SUB)
                for s in range(SUB):
                    last = v.tensor_scalar(pxn[:, s, :], px[r][:, s, :], pmv[:, s, 0:1], prstd[:, s:s + 1], ALU.subtract, ALU.mult)
                last.then_inc(p_xn, 1)

            def split(g, r):
                dve.wait_ge(p_qkf, g + 1)
                need(dve, qk_stored[r], 16 * 2 * PARTS * (g // 2) if isinstance(g, int) else 16 * PARTS * (g - r))
                v.tensor_copy(pparts[r][:, 0, :, :], pqk).then_inc(p_split, 1)
                dve.wait_ge(p_split, 4 * g + 1)
                v.tensor_tensor(pres, pqk, pparts[r][:, 0, :, :], ALU.subtract).then_inc(p_split, 1)
                dve.wait_ge(p_split, 4 * g + 2)
                v.tensor_copy(pparts[r][:, 1, :, :], pres).then_inc(p_split, 1)
                dve.wait_ge(p_split, 4 * g + 3)
                v.tensor_tensor(pparts[r][:, 2, :, :], pres, pparts[r][:, 1, :, :], ALU.subtract).then_inc(p_split, 1)

            norm(0, 0)
            for g in range(2):
                norm(g + 1, 1 - g)
                split(g, g)
            with dve.Fori(2, NG - 2, 2) as g:
                norm(g + 1, 1)
                split(g, 0)
                norm(g + 2, 0)
                split(g + 1, 1)
            norm(NG - 1, 1)
            split(NG - 2, 0)
            split(NG - 1, 1)

            def ffn_stats_of(n, par, done, count):
                dve.wait_ge(done, count)
                v.bn_stats(st[:, 0, :], xin[:, par, :]).then_inc(ffn_stats, 1)

            def ffn_mean(n):
                stand_alone(dve, (ffn_stats, n + 1), (ffn_xn, n))
                v.bn_aggr(mv[:, 0, :], st[:, 0, :]).then_inc(ffn_mv, 1)

            def ffn_result(n, par, stored, count):
                dve.wait_ge(lif, LIF_OPS * (n + 1))
                need(dve, stored, count)
                v.scalar_tensor_tensor(out=xout[:, par, :], in0=cnt[:, :], scalar=1.0 / STEPS, in1=xin[:, par, :],
                                       op0=ALU.mult, op1=ALU.add).then_inc(ffn_out, 1)

            def row_min(i, par, half):
                t0 = HALF * half
                dve.wait_ge(max_b, CPT * i + CPT // 2 * (half + 1))
                need(dve, w_dlt, 2 * i + half)
                if isinstance(i, int) and i == 0:
                    dve.wait_ge(att_dlt, T)
                v.tensor_tensor(nrow[:, 0:HALF], nmax[:, par, t0:t0 + HALF, 0], nmax[:, par, t0:t0 + HALF, 1], ALU.min) \
                    .then_inc(w_min, 1)

            def row_rec(i, half):
                dve.wait_ge(w_sum, 2 * (2 * i + half) + 2)
                if isinstance(i, int) and i == 0:
                    dve.wait_ge(att_step, 2 * T)
                v.reciprocal(rec[:, 0:HALF], tot[:, 0:HALF]).then_inc(w_rec, 1)

            def head_maxima(i, par, c):
                if c == 0:
                    need(dve, w_dlt, 2 * (i - 1))
                    if isinstance(i, int) and i == 0:
                        dve.wait_ge(att_dlt, T - 1)
                dve.wait_ge(scores_b, CPT * i + c + 1)
                v.tensor_reduce(nmax[:, par, c // NCH, c % NCH:c % NCH + 1], score[buffers_b[CPT * par + c][0]][:, :],
                                AX.X, ALU.max, negate=True).then_inc(max_b, 1)
                if c == 15:
                    row_min(i, par, 0)
                if c == 18:
                    row_rec(i, 0)
                if c == 31:
                    row_min(i, par, 1)

            def phase_a(it, par, _):
                i, i1, i2, i3 = (tile_at(it, n) for n in range(4))
                r1, r3 = 1 - par, 1 - par
                for c in range(CPT):
                    if i is not None:
                        if c == 0:
                            need(dve, att_dlt, i - 1)
                        dve.wait_ge(scores_a, CPT * i + c + 1)
                        v.tensor_reduce(nmax[:, par, c // NCH, c % NCH:c % NCH + 1], score[buffers_a[CPT * par + c][0]][:, :],
                                        AX.X, ALU.max, negate=True).then_inc(max_a, 1)
                    elif head0(it):
                        head_maxima(0, 0, c)
                    if i1 is not None:
                        if c == 0:
                            dve.wait_ge(max_a, CPT * i1 + CPT)
                            need(dve, att_dlt, i1)
                            v.tensor_tensor(nrow[:, :], nmax[:, r1, :, 0], nmax[:, r1, :, 1], ALU.min).then_inc(att_min, 1)
                        if c == 4:
                            dve.wait_ge(att_sum, 2 * i1 + 2)
                            v.reciprocal(rec[:, :], tot[:, :]).then_inc(att_rec, 1)
                        if c == 11:
                            dve.wait_ge(oproj, i1 + 1)
                            need(dve, ffn_out, i1 - 1)
                            if isinstance(i1, int):
                                dve.wait_ge(xv_loaded[r1], 32 * (i1 // 2 + 1))
                            else:
                                dve.wait_ge(xv_loaded[r1], 16 * (i1 - r1) + 32)
                            v.tensor_tensor(xin[:, r1, :], bank_f[:, D:2 * D], xa[:, r1, :], ALU.add).then_inc(ffn_x1, 1)
                        if c == 12:
                            ffn_stats_of(i1, r1, ffn_x1, i1 + 1)
                        if c == 13:
                            ffn_mean(i1)
                    if i3 is not None and c == 5:
                        need(dve, qkv_xn, i3 - 1)
                        ffn_result(i3, r3, x2_stored[r3], 8 * (i3 - r3))
                    if i3 is not None and c == 6:
                        dve.wait_ge(ffn_out, i3 + 1)
                        v.bn_stats(st[:, 1, :], xout[:, r3, :]).then_inc(qkv_stats, 1)
                    if i3 is not None and c == 7:
                        stand_alone(dve, (qkv_stats, i3 + 1), (qkv_xn, i3))
                        v.bn_aggr(mv[:, 1, :], st[:, 1, :]).then_inc(qkv_mv, 1)
                    if c == 8 and last_tile(i2):
                        neuron(dve, v, i2, par, 1, LIF_OPS)
            iterations(dve, phase_a)

            def phase_b(it, par, _):
                i, i1, i2, i3 = (tile_at(it, n) for n in range(4))
                for c in range(CPT):
                    if i is not None:
                        head_maxima(i, par, c)
                    if i1 is not None:
                        if c == 2:
                            row_rec(i1, 1)
                        for sc in range(4):
                            if c == PROD_AT[0][2 * sc + 1]:
                                dve.wait_ge(prod_ready, 8 * i1 + 4 + sc + 1)
                                dve.wait_ge(prod_kept, 4 * i1 + sc + 1)
                                cols = prod[:, sc * BANK:(sc + 1) * BANK]
                                v.tensor_tensor(cols, bank_g[:, :], cols, ALU.add).then_inc(prod_added, 1)
                        if c == 24:
                            ffn_stats_of(T + i1, 1 - par, x3_ready, i1 + 1)
                        if c == 25:
                            ffn_mean(T + i1)
                    if i3 is not None and c == 20:
                        if isinstance(i3, int) and i3 < 2:
                            dve.wait_ge(x2_stored[1 - par], 16 * T // 2)
                            dve.wait_ge(qkv_xn, T)
                        ffn_result(T + i3, 1 - par, out_stored[1 - par], 8 * (i3 - (1 - par)))
                    if c == 22 and i2 is not None and last_tile(T + i2):
                        neuron(dve, v, T + i2, par, 1, LIF_OPS)
            iterations(dve, phase_b, first=1)

        @block.scalar
        def _(act):
            a = nc.scalar
            act.wait_ge(bq_ready, 1)
            act.wait_ge(w_in_loaded, 16 * N_PRELUDE_LOADS)

            def group(g):
                act.wait_ge(p_tr, g + 1)
                need(act, p_v, g)
                for k in range(KC):
                    last = a.activation(pxT[:, k, :], score[0][:, k * GROUP:(k + 1) * GROUP], ACT.Copy)
                last.then_inc(p_xT, 1)
                need(act, p_split, 4 * g - 2)
                for m in range(2 * KC):
                    act.wait_ge(p_qk, 4 * g + m + 1)
                    src = score[1 + m // 2][:, (m % 2) * GROUP:(m % 2 + 1) * GROUP]
                    if m < KC:
                        last = a.activation(pqk[:, m, :], src, ACT.Identity, bias=bq_scaled[:, m:m + 1], scale=DH ** -0.5)
                    else:
                        last = a.activation(pqk[:, m, :], src, ACT.Identity, bias=bin_col[:, m:m + 1])
                last.then_inc(p_qkf, 1)
                act.wait_ge(p_v, g + 1)
                need(act, v_stored, 16 * g)
                a.activation(pv_sb[:, 0:2, :], bank_f[:, :].rearrange("p (s d) -> p s d", s=2), ACT.Copy)
                a.activation(pv_sb[:, 2:4, :], bank_g[:, :].rearrange("p (s d) -> p s d", s=2), ACT.Copy).then_inc(p_vs, 1)
            group(0)
            with act.Fori(1, NG) as g:
                group(g)

            def ffn_columns(n):
                act.wait_ge(ffn_tr, n + 1)
                need(act, ffn_fc, 2 * n)
                a.activation(xnT[:, :, :], bank_f[:, 0:D].rearrange("p (k n) -> p k n", k=KC), ACT.Copy).then_inc(ffn_xT, 1)

            def ffn_act(n, part):
                act.wait_ge(ffn_fc, 2 * n + part + 1)
                if part == 0:
                    need(act, ffn_y, n)
                a.activation(hid[:, part * BANK:(part + 1) * BANK], bank_f[:, :], ACT.Relu).then_inc(ffn_relu, 1)

            def ffn_take(n, r):
                act.wait_ge(ffn_y, n + 1)
                need(act, lif, LIF_OPS * (n - 1))
                a.activation(y[:, r, :], bank_f[:, 0:D], ACT.Copy).then_inc(ffn_ysb, 1)

            def row_fac(i, half):
                act.wait_ge(w_dlt, 2 * i + half + 1)
                need(act, w_qw, 2 * i + half)
                if isinstance(i, int) and i == 0:
                    act.wait_ge(att_sum, 2 * T)
                a.activation(fac[:, 0:HALF, :], dlt[:, 0:HALF, :], ACT.Exp).then_inc(w_fac, 1)

            def keep_product(i, sc):
                act.wait_ge(prod_ready, 8 * i + sc + 1)
                need(act, pieces_loaded, 16 * 4 * i)
                a.activation(prod[:, sc * BANK:(sc + 1) * BANK], bank_g[:, :], ACT.Copy).then_inc(prod_kept, 1)

            def head_exp(i, par, c):
                if c == 0:
                    need(act, w_sum, 2 * 2 * (i - 1))
                    if isinstance(i, int) and i == 0:
                        act.wait_ge(att_sum, 2 * (T - 1))
                    need(act, prod_ready, 8 * (i - 1) + 4)
                if c == CPT // 2:
                    need(act, prod_ready, 8 * i)
                act.wait_ge(max_b, CPT * i + c + 1)
                a.activation(expo[:, c // NCH, (c % NCH) * CH:(c % NCH + 1) * CH], score[buffers_b[CPT * par + c][0]][:, :],
                             ACT.Exp, bias=nmax[:, par, c // NCH, c % NCH:c % NCH + 1],
                             accum_out=esum[:, par, c // NCH, c % NCH:c % NCH + 1]).then_inc(exp_b, 1)
                if c == 15:
                    row_fac(i, 0)
                if c == 31:
                    row_fac(i, 1)
                for sc in range(4):
                    if c == PROD_AT[1][2 * sc + 1] - 1 and (sc < 3 or isinstance(i, int) and i == 0):
                        keep_product(i, sc)

            act.wait_ge(w_loaded, 16 * N_WEIGHT_LOADS)

            def phase_a(it, par, _):
                i, i1, i3 = tile_at(it, 0), tile_at(it, 1), tile_at(it, 3)
                for c in range(CPT):
                    if i is not None:
                        if c == 0:
                            need(act, att_sum, 2 * (i - 1))
                        act.wait_ge(max_a, CPT * i + c + 1)
                        s = score[buffers_a[CPT * par + c][0]]
                        a.activation(s[:, :], s[:, :], ACT.Exp, bias=nmax[:, par, c // NCH, c % NCH:c % NCH + 1],
                                     accum_out=esum[:, par, c // NCH, c % NCH:c % NCH + 1]).then_inc(exp_a, 1)
                    elif head0(it):
                        head_exp(0, 0, c)
                    if i1 is not None:
                        if c == 1:
                            act.wait_ge(att_dlt, i1 + 1)
                            need(act, att_sum, 2 * i1)
                            a.activation(fac[:, :, :], dlt[:, :, :], ACT.Exp).then_inc(att_fac, 1)
                        if c == 7:
                            act.wait_ge(opt_tr, i1 + 1)
                            a.activation(optT[:, :, :], bank_f[:, 0:D].rearrange("p (k n) -> p k n", k=KC), ACT.Copy) \
                                .then_inc(opt_T, 1)
                        if c == 15:
                            ffn_columns(i1)
                        if c == 19:
                            ffn_act(i1, 0)
                        if c == 23:
                            ffn_act(i1, 1)
                        if c == 29:
                            ffn_take(i1, 1 - par)
                    if i3 is not None:
                        r = 1 - par
                        if c == 10:
                            act.wait_ge(qkv_tr, i3 + 1)
                            need(act, qkv_q, i3)
                            a.activation(xn2T[:, :, :], bank_g[:, 0:D].rearrange("p (k n) -> p k n", k=KC), ACT.Copy) \
                                .then_inc(qkv_xT, 1)
                        if c == 15:
                            act.wait_ge(qkv_kv, i3 + 1)
                            need(act, qkv_split, 4 * i3)
                            a.activation(kvf[:, 0:D], bank_g[:, 0:D], ACT.Copy, scale=temp_sb[:, bass.ds(i3, 1)])
                            a.activation(kvf[:, D:2 * D], bank_g[:, D:2 * D], ACT.Copy).then_inc(qkv_kvf, 1)
                        if c == 20:
                            act.wait_ge(qkv_q, i3 + 1)
                            need(act, qb_stored[r], 8 * (i3 - r))
                            for m in range(KC):
                                last = a.activation(attention_q(i3, r)[:, m * P:(m + 1) * P], bank_g[:, m * P:(m + 1) * P],
                                                    ACT.Identity, bias=bqb_col[:, m:m + 1])
                            last.then_inc(qkv_qf, 1)
            iterations(act, phase_a)

            def phase_b(it, par, _):
                i, i1, i2 = tile_at(it, 0), tile_at(it, 1), tile_at(it, 2)
                for c in range(CPT):
                    if i is not None:
                        head_exp(i, par, c)
                    if i1 is not None and c == 2 and not (isinstance(i1, int) and i1 == 0):
                        keep_product(i1, 3)
                    if i2 is not None:
                        if c == 1:
                            ffn_columns(T + i2)
                        if c == 4:
                            ffn_act(T + i2, 0)
                        if c == 13:
                            ffn_act(T + i2, 1)
                        if c == 20:
                            ffn_take(T + i2, par)
            iterations(act, phase_b, first=1)

        @block.gpsimd
        def _(pool):
            g_ = nc.gpsimd
            g_.memset(ident[:, :], 0.0).then_inc(ident0, 1)
            pool.wait_ge(ident0, 1)
            g_.affine_select(out=ident[:, :], in_=ident[:, :], compare_op=ALU.not_equal, fill=1.0, base=0,
                             pattern=[[-1, P]], channel_multiplier=1).then_inc(consts, 1)
            pool.wait_ge(consts, 4)

            def group_rstd(g):
                stand_alone(pool, (p_aggr, SUB * g + SUB), (p_xn, g))
                g_.tensor_scalar(pvar, pmv[:, :, 1], EPS, 0.0, ALU.add, ALU.add).then_inc(p_rstd, 1)
                pool.wait_ge(p_rstd, 2 * g + 1)
                g_.tensor_tensor(prstd, pvar, power[:, 0:SUB], ALU.pow).then_inc(p_rstd, 1)
            group_rstd(0)
            with pool.Fori(1, NG) as g:
                group_rstd(g)

            def normalise(n, which, got, step, dst, src, free, count):
                stand_alone(pool, (got, n + 1))
                g_.tensor_scalar(var[:, which:which + 1], mv[:, which, 1:2], EPS, 0.0, ALU.add, ALU.add).then_inc(step, 1)
                pool.wait_ge(step, 2 * n + 1)
                g_.tensor_tensor(rstd[:, which:which + 1], var[:, which:which + 1], power[:, 0:1], ALU.pow).then_inc(step, 1)
                stand_alone(pool, (step, 2 * n + 2), (free, count))
                return g_.tensor_scalar(dst, src, mv[:, which, 0:1], rstd[:, which:which + 1], ALU.subtract, ALU.mult)

            def square(n, part):
                pool.wait_ge(ffn_relu, 2 * n + part + 1)
                h = hid[:, part * BANK:(part + 1) * BANK]
                g_.tensor_tensor(h, h, h, ALU.mult).then_inc(ffn_sq, 1)

            def spikes(n, r, first, last):
                if not last_tile(n):
                    neuron(pool, g_, n, r, first, last)

            def spread(ap, m):
                return ap.unsqueeze(2).broadcast_to([P, ap.shape[1], m])

            def half_distance(i, par, half):
                n, t0 = 2 * i + half, HALF * half
                pool.wait_ge(w_min, n + 1)
                g_.tensor_tensor(dlt[:, 0:HALF, :], spread(nrow[:, 0:HALF], NCH), nmax[:, par, t0:t0 + HALF, :], ALU.subtract) \
                    .then_inc(w_dlt, 1)

            def half_sums(i, par, half):
                n, t0 = 2 * i + half, HALF * half
                pool.wait_ge(w_fac, n + 1)
                pool.wait_ge(exp_b, CPT * i + CPT // 2 * (half + 1))
                g_.tensor_tensor(sume[:, 0:HALF, :], esum[:, par, t0:t0 + HALF, :], fac[:, 0:HALF, :], ALU.mult).then_inc(w_sum, 1)
                pool.wait_ge(w_sum, 2 * n + 1)
                g_.tensor_tensor(tot[:, 0:HALF], sume[:, 0:HALF, 0], sume[:, 0:HALF, 1], ALU.add).then_inc(w_sum, 1)

            def weigh_q(i, par, half):
                n = 2 * i + half
                pool.wait_ge(w_rec, n + 1)
                g_.tensor_tensor(wgt[:, 0:HALF, :], fac[:, 0:HALF, :], spread(rec[:, 0:HALF], NCH), ALU.mult).then_inc(w_step, 1)
                pool.wait_ge(w_step, n + 1)
                need(pool, prod_ready, 4 * n)
                q = qcol[:, par, :].rearrange("p (m j r) -> p r m j", m=KC, r=8)
                for c in range(NCH):
                    last = g_.tensor_tensor(qw[:, c, :, 0:DH].rearrange("p (r m) j -> p r m j", m=KC),
                                            q[:, 4 * half:4 * half + 4, :, :],
                                            wgt[:, 0:HALF, c].rearrange("p (r m) -> p r m", m=KC).unsqueeze(3)
                                            .broadcast_to([P, 4, KC, DH]), ALU.mult)
                last.then_inc(w_qw, 1)

            def row_distance(i, par):
                pool.wait_ge(att_min, i + 1)
                g_.tensor_tensor(dlt[:, :, :], spread(nrow[:, :], NCH), nmax[:, par, :, :], ALU.subtract).then_inc(att_dlt, 1)

            def row_sums(i, par):
                pool.wait_ge(att_fac, i + 1)
                pool.wait_ge(exp_a, CPT * i + CPT)
                g_.tensor_tensor(sume[:, :, :], esum[:, par, :, :], fac[:, :, :], ALU.mult).then_inc(att_sum, 1)
                pool.wait_ge(att_sum, 2 * i + 1)
                g_.tensor_tensor(tot[:, :], sume[:, :, 0], sume[:, :, 1], ALU.add).then_inc(att_sum, 1)

            def row_output(i, par):
                pool.wait_ge(att_rec, i + 1)
                g_.tensor_tensor(wgt[:, :, :], sume[:, :, :], spread(rec[:, :], NCH), ALU.mult).then_inc(att_step, 1)
                pool.wait_ge(att_step, 2 * i + 1)
                g_.tensor_tensor(wsum[:, :], wgt[:, :, 0], wgt[:, :, 1], ALU.add).then_inc(att_step, 1)
                pool.wait_ge(att_step, 2 * i + 2)
                if isinstance(i, int):
                    pool.wait_ge(xv_loaded[par], 32 * (i // 2 + 1))
                else:
                    pool.wait_ge(xv_loaded[par], 16 * (i - par) + 32)
                need(pool, opt_tr, i)
                g_.tensor_tensor(opt.rearrange("p (h d) -> p h d", h=H), va[:, par, :].rearrange("p (h d) -> p h d", h=H),
                                 spread(wsum[:, :], DH), ALU.mult).then_inc(att_opt, 1)

            def split_kv(i):
                stand_alone(pool, (qkv_kvf, i + 1), (parts_stored, 16 * 2 * PARTS * i))
                g_.tensor_scalar(kvparts[:, 0, :], kvf, 1.0, 0.0, ALU.mult, ALU.add).then_inc(qkv_split, 1)
                pool.wait_ge(qkv_split, 4 * i + 1)
                g_.tensor_tensor(kvres, kvf, kvparts[:, 0, :], ALU.subtract).then_inc(qkv_split, 1)
                stand_alone(pool, (qkv_split, 4 * i + 2))
                g_.tensor_scalar(kvparts[:, 1, :], kvres, 1.0, 0.0, ALU.mult, ALU.add).then_inc(qkv_split, 1)
                pool.wait_ge(qkv_split, 4 * i + 3)
                g_.tensor_tensor(kvparts[:, 2, :], kvres, kvparts[:, 1, :], ALU.subtract).then_inc(qkv_split, 1)

            def phase_a(it, par, _):
                i1, i2, i3 = (tile_at(it, n) for n in (1, 2, 3))
                if i1 is not None:
                    row_distance(i1, 1 - par)
                if i3 is not None:
                    spikes(i3, 1 - par, 20, LIF_OPS)
                if i1 is not None:
                    row_sums(i1, 1 - par)
                if i2 is not None:
                    spikes(i2, par, 1, 1)
                if i1 is not None:
                    row_output(i1, 1 - par)
                if i3 is not None:
                    normalise(i3, 1, qkv_mv, qkv_step, xn2, xout[:, 1 - par, :], qkv_tr, i3).then_inc(qkv_xn, 1)
                if i2 is not None:
                    spikes(i2, par, 2, 5)
                if i1 is not None:
                    normalise(i1, 0, ffn_mv, ffn_step, xn[:, :], xin[:, 1 - par, :], ffn_tr, i1).then_inc(ffn_xn, 1)
                if i2 is not None:
                    spikes(i2, par, 6, 7)
                if head0(it):
                    half_distance(0, 0, 0)
                    half_sums(0, 0, 0)
                    weigh_q(0, 0, 0)
                if i3 is not None:
                    split_kv(i3)
                if i1 is not None:
                    square(i1, 0)
                if i2 is not None:
                    spikes(i2, par, 8, 10)
                if i1 is not None:
                    square(i1, 1)
                if i2 is not None:
                    spikes(i2, par, 11, 19)
                if head0(it):
                    half_distance(0, 0, 1)
            iterations(pool, phase_a)

            def add_pieces(i, par):
                pool.wait_ge(x2_loaded, 16 * (i + 1))
                pool.wait_ge(pieces_loaded, 16 * 4 * (i + 1))
                need(pool, ffn_out, T + i - 1)
                for g in range(4):
                    src = x2_in[:, :] if g == 0 else xin[:, par, :]
                    ins = g_.tensor_tensor(xin[:, par, :], src, pieces[:, g, :], ALU.add)
                    if g < 3:
                        ins.then_inc(x3_step, 1)
                        pool.wait_ge(x3_step, 3 * i + g + 1)
                ins.then_inc(x3_ready, 1)

            def phase_b(it, par, _):
                i, i1, i2, i3 = (tile_at(it, n) for n in range(4))
                if i1 is not None:
                    half_sums(i1, 1 - par, 1)
                if i3 is not None:
                    spikes(T + i3, 1 - par, 7, 8)
                if i1 is not None:
                    weigh_q(i1, 1 - par, 1)
                if i3 is not None:
                    spikes(T + i3, 1 - par, 9, 9)
                if i2 is not None:
                    square(T + i2, 0)
                if i3 is not None:
                    spikes(T + i3, 1 - par, 10, 18)
                if i2 is not None:
                    square(T + i2, 1)
                if i is not None:
                    half_distance(i, par, 0)
                if i3 is not None:
                    spikes(T + i3, 1 - par, 19, 19)
                if i is not None:
                    half_sums(i, par, 0)
                if i3 is not None:
                    spikes(T + i3, 1 - par, 20, 20)
                if i is not None:
                    weigh_q(i, par, 0)
                if i3 is not None:
                    spikes(T + i3, 1 - par, 21, LIF_OPS)
                if i1 is not None:
                    add_pieces(i1, 1 - par)
                if i2 is not None:
                    spikes(T + i2, par, 1, 2)
                if i1 is not None:
                    normalise(T + i1, 0, ffn_mv, ffn_step, xn[:, :], xin[:, 1 - par, :], ffn_tr, T + i1).then_inc(ffn_xn, 1)
                if i2 is not None:
                    spikes(T + i2, par, 3, 6)
                if i is not None:
                    half_distance(i, par, 1)
            iterations(pool, phase_b, first=1)


_NAMES = ["x", "w_in", "b_in_col", "b_in_row", "w_out", "b_out", "wq", "bq_col", "wkv", "bkv_row", "temp", "w_fc", "w_proj"]


def kernel(**inputs):
    import numpy as np
    import concourse.bacc as bacc
    from concourse.bass_utils import run_bass_kernel_spmd as run

    a = {n: np.asarray(v) for n, v in inputs.items()}
    w_in = a["L0_attn_a_w_in"].reshape(H, 3, DH, D).transpose(1, 0, 2, 3).reshape(3 * D, D)
    b_in = a["L0_attn_a_b_in"].reshape(H, 3, DH).transpose(1, 0, 2).reshape(3 * D)
    laid = {
        "x": a["L0_attn_a_x"].reshape(TOK, D),
        "w_in": w_in.T,
        "b_in_col": b_in[:2 * D].reshape(2 * KC, P).T,
        "b_in_row": b_in[2 * D:].reshape(1, D),
        "w_out": a["L0_attn_a_w_out"].T,
        "b_out": a["L0_attn_a_b_out"].reshape(1, D),
        "wq": a["L0_attn_b_Wq"],
        "bq_col": a["L0_attn_b_bq"].reshape(KC, P).T,
        "wkv": np.concatenate([a["L0_attn_b_Wk"], a["L0_attn_b_Wv"]], axis=1),
        "bkv_row": np.concatenate([a["L0_attn_b_bk"], a["L0_attn_b_bv"]]).reshape(1, 2 * D),
        "temp": a["L0_attn_b_temperature"].reshape(1, H),
        "w_fc": a["L0_ffn_W_fc"].T,
        "w_proj": a["L0_ffn_W_proj"].T,
    }
    nc = bacc.Bacc("TRN2", target_bir_lowering=False, num_devices=1)
    arrays, args = {}, []
    for name in _NAMES:
        arrays["in_" + name] = np.ascontiguousarray(laid[name])
        args.append(nc.dram_tensor("in_" + name, arrays["in_" + name].shape, FP32, kind="ExternalInput").ap())
    out = nc.dram_tensor("out", (BATCH, SEQ, D), FP32, kind="ExternalOutput").ap()
    build(nc, *args, out.rearrange("b l d -> (b l) d"))
    r = run(nc, [arrays], core_ids=[0])
    return r.results[0]["out"]
```
